# Optimizing a Trainium2 kernel written in Bass

```python
import numpy as np
import jax
import jax.numpy as jnp

def _softmax(x, axis=-1):
    return jax.nn.softmax(x, axis=axis)

def _gelu(x):
    return jax.nn.gelu(x, approximate=True)

def _silu(x):
    return jax.nn.silu(x)

def _sigmoid(x):
    return jax.nn.sigmoid(x)

def _layernorm(x, axis=-1, eps=1e-05):
    m = jnp.mean(x, axis=axis, keepdims=True)
    v = jnp.var(x, axis=axis, keepdims=True)
    return (x - m) / jnp.sqrt(v + eps)

def _scatter_add(tgt, idx, src, axis=0):
    return tgt.at[idx].add(src)

def _segment_sum(src, seg, n):
    return jax.ops.segment_sum(src, seg, n)
kernel_name = 'mk_sandwich_d1_jaxref_r8_26290e'

def setup_inputs(seed: int=0):
    np.random.seed(seed)
    _w = jnp.asarray

    def _L0_attn_setup():
        import jax, jax.numpy as jnp
        import numpy as np
        import math
        HIDDEN = 256
        NUM_HEADS = 16
        NUM_KV_HEADS = 4
        HEAD_DIM = 128
        GROUPS = NUM_HEADS // NUM_KV_HEADS
        BATCH = 1
        SEQ = 512
        THETA = 10000.0

        def _rope(x):
            seq = x.shape[2]
            freqs = 1.0 / THETA ** (jnp.arange(0, HEAD_DIM, 2, dtype=jnp.float32) / HEAD_DIM)
            angles = jnp.arange(seq, dtype=jnp.float32)[:, None] * freqs[None, :]
            cos = jnp.cos(angles)[None, None]
            sin = jnp.sin(angles)[None, None]
            x1 = x[..., 0::2]
            x2 = x[..., 1::2]
            rot = jnp.stack([x1 * cos - x2 * sin, x1 * sin + x2 * cos], axis=-1)
            return rot.reshape(x.shape)
        key = jax.random.key(seed)
        kx, kq, kk, kv, ko = jax.random.split(key, 5)
        scale = 0.02
        x = jax.random.normal(kx, (BATCH, SEQ, HIDDEN), dtype=jnp.float32)
        Wq = jax.random.normal(kq, (NUM_HEADS * HEAD_DIM, HIDDEN), dtype=jnp.float32) * scale
        Wk = jax.random.normal(kk, (NUM_KV_HEADS * HEAD_DIM, HIDDEN), dtype=jnp.float32) * scale
        Wv = jax.random.normal(kv, (NUM_KV_HEADS * HEAD_DIM, HIDDEN), dtype=jnp.float32) * scale
        Wo = jax.random.normal(ko, (HIDDEN, NUM_HEADS * HEAD_DIM), dtype=jnp.float32) * scale
        return {'x': x, 'Wq': Wq, 'Wk': Wk, 'Wv': Wv, 'Wo': Wo}
    _L0_attn_in = _L0_attn_setup()

    def _L0_ffn_setup():
        import jax, jax.numpy as jnp
        import numpy as np
        E, K, H, F = (64, 6, 256, 96)
        G, KG = (8, 4)
        SHARED_F = 96
        SCALE = 2.5
        T = 2 * 128
        CAP = 2 * (T * K // E)

        def _grouped_topk(logits, bias):
            scores = jax.nn.sigmoid(logits.astype(jnp.float32))
            scores_b = scores + bias[None, :]
            gs = scores_b.reshape(-1, G, E // G)
            group_scores = jnp.sum(jax.lax.top_k(gs, 2)[0], axis=-1)
            gidx = jax.lax.top_k(group_scores, KG)[1]
            rows = jnp.arange(group_scores.shape[0])[:, None]
            group_mask = jnp.zeros_like(group_scores).at[rows, gidx].set(1.0)
            score_mask = jnp.repeat(group_mask, E // G, axis=-1) > 0
            tmp = jnp.where(score_mask, scores_b, -jnp.inf)
            topk_ids = jax.lax.top_k(tmp, K)[1]
            topk_w = jnp.take_along_axis(scores, topk_ids, axis=-1)
            topk_w = topk_w / jnp.sum(topk_w, axis=-1, keepdims=True)
            return (topk_w * SCALE, topk_ids)

        def _routed_moe(x, topk_w, topk_ids, w_gate, w_up, w_down):
            Tn = x.shape[0]
            flat_e = topk_ids.reshape(-1)
            order = jnp.argsort(flat_e)
            se = flat_e[order]
            pos = jnp.arange(Tn * K) - jnp.searchsorted(se, se, side='left')
            tok = order // K
            valid = pos < CAP
            slot = jnp.where(valid, pos, CAP)
            buf = jnp.zeros((E, CAP + 1, H), x.dtype).at[se, slot].set(x[tok])[:, :CAP]
            h = jax.nn.silu(jnp.einsum('ech,ehf->ecf', buf, w_gate)) * jnp.einsum('ech,ehf->ecf', buf, w_up)
            out = jnp.einsum('ecf,efh->ech', h, w_down)
            gathered = out[se, jnp.minimum(pos, CAP - 1)] * valid.astype(x.dtype)[:, None]
            w = topk_w.reshape(-1)[order].astype(x.dtype)[:, None]
            return jax.ops.segment_sum(gathered * w, tok, num_segments=Tn)
        key = jax.random.key(seed)
        ks = jax.random.split(key, 9)
        s = 0.02
        return dict(hidden_states=jax.random.normal(ks[0], (2, 128, H), jnp.float32), gate_w=jax.random.normal(ks[1], (H, E), jnp.float32) * s, bias=jax.random.normal(ks[2], (E,), jnp.float32) * s, w_gate=jax.random.normal(ks[3], (E, H, F), jnp.float32) * s, w_up=jax.random.normal(ks[4], (E, H, F), jnp.float32) * s, w_down=jax.random.normal(ks[5], (E, F, H), jnp.float32) * s, ws_gate=jax.random.normal(ks[6], (H, SHARED_F), jnp.float32) * s, ws_up=jax.random.normal(ks[7], (H, SHARED_F), jnp.float32) * s, ws_down=jax.random.normal(ks[8], (SHARED_F, H), jnp.float32) * s)
    _L0_ffn_in = _L0_ffn_setup()
    _d = {'L0_attn_x': _L0_attn_in['x'], 'L0_attn_Wq': _L0_attn_in['Wq'], 'L0_attn_Wk': _L0_attn_in['Wk'], 'L0_attn_Wv': _L0_attn_in['Wv'], 'L0_attn_Wo': _L0_attn_in['Wo'], 'L0_ffn_gate_w': _L0_ffn_in['gate_w'], 'L0_ffn_bias': _L0_ffn_in['bias'], 'L0_ffn_w_gate': _L0_ffn_in['w_gate'], 'L0_ffn_w_up': _L0_ffn_in['w_up'], 'L0_ffn_w_down': _L0_ffn_in['w_down'], 'L0_ffn_ws_gate': _L0_ffn_in['ws_gate'], 'L0_ffn_ws_up': _L0_ffn_in['ws_up'], 'L0_ffn_ws_down': _L0_ffn_in['ws_down']}
    _x0 = _d['L0_attn_x']
    _d['L0_attn_x'] = jax.random.normal(jax.random.fold_in(jax.random.key(seed), 1), (4, 1024, 256), dtype=_x0.dtype)
    del _x0
    return _d

def reference(L0_attn_x, L0_attn_Wq, L0_attn_Wk, L0_attn_Wv, L0_attn_Wo, L0_ffn_gate_w, L0_ffn_bias, L0_ffn_w_gate, L0_ffn_w_up, L0_ffn_w_down, L0_ffn_ws_gate, L0_ffn_ws_up, L0_ffn_ws_down):

    def _L0_attn_ref(x, Wq, Wk, Wv, Wo):
        import jax, jax.numpy as jnp
        import numpy as np
        import math
        HIDDEN = 256
        NUM_HEADS = 16
        NUM_KV_HEADS = 4
        HEAD_DIM = 128
        GROUPS = NUM_HEADS // NUM_KV_HEADS
        BATCH = 1
        SEQ = 512
        THETA = 10000.0

        def _rope(x):
            seq = x.shape[2]
            freqs = 1.0 / THETA ** (jnp.arange(0, HEAD_DIM, 2, dtype=jnp.float32) / HEAD_DIM)
            angles = jnp.arange(seq, dtype=jnp.float32)[:, None] * freqs[None, :]
            cos = jnp.cos(angles)[None, None]
            sin = jnp.sin(angles)[None, None]
            x1 = x[..., 0::2]
            x2 = x[..., 1::2]
            rot = jnp.stack([x1 * cos - x2 * sin, x1 * sin + x2 * cos], axis=-1)
            return rot.reshape(x.shape)
        B, S, _ = x.shape
        q = (x @ Wq.T).reshape(B, S, NUM_HEADS, HEAD_DIM).transpose(0, 2, 1, 3)
        k = (x @ Wk.T).reshape(B, S, NUM_KV_HEADS, HEAD_DIM).transpose(0, 2, 1, 3)
        v = (x @ Wv.T).reshape(B, S, NUM_KV_HEADS, HEAD_DIM).transpose(0, 2, 1, 3)
        q = _rope(q)
        k = _rope(k)
        k = jnp.repeat(k, GROUPS, axis=1)
        v = jnp.repeat(v, GROUPS, axis=1)
        scale = 1.0 / math.sqrt(HEAD_DIM)
        scores = jnp.einsum('bhqd,bhkd->bhqk', q, k) * scale
        causal = jnp.triu(jnp.ones((S, S), dtype=bool), k=1)
        scores = jnp.where(causal[None, None], jnp.float32(-jnp.inf), scores)
        attn = jax.nn.softmax(scores, axis=-1)
        out = jnp.einsum('bhqk,bhkd->bhqd', attn, v)
        out = out.transpose(0, 2, 1, 3).reshape(B, S, NUM_HEADS * HEAD_DIM)
        return out @ Wo.T

    def _L0_ffn_ref(hidden_states, gate_w, bias, w_gate, w_up, w_down, ws_gate, ws_up, ws_down):
        import jax, jax.numpy as jnp
        import numpy as np
        E, K, H, F = (64, 6, 256, 96)
        G, KG = (8, 4)
        SHARED_F = 96
        SCALE = 2.5
        T = 2 * 128
        CAP = 2 * (T * K // E)

        def _grouped_topk(logits, bias):
            scores = jax.nn.sigmoid(logits.astype(jnp.float32))
            scores_b = scores + bias[None, :]
            gs = scores_b.reshape(-1, G, E // G)
            group_scores = jnp.sum(jax.lax.top_k(gs, 2)[0], axis=-1)
            gidx = jax.lax.top_k(group_scores, KG)[1]
            rows = jnp.arange(group_scores.shape[0])[:, None]
            group_mask = jnp.zeros_like(group_scores).at[rows, gidx].set(1.0)
            score_mask = jnp.repeat(group_mask, E // G, axis=-1) > 0
            tmp = jnp.where(score_mask, scores_b, -jnp.inf)
            topk_ids = jax.lax.top_k(tmp, K)[1]
            topk_w = jnp.take_along_axis(scores, topk_ids, axis=-1)
            topk_w = topk_w / jnp.sum(topk_w, axis=-1, keepdims=True)
            return (topk_w * SCALE, topk_ids)

        def _routed_moe(x, topk_w, topk_ids, w_gate, w_up, w_down):
            Tn = x.shape[0]
            flat_e = topk_ids.reshape(-1)
            order = jnp.argsort(flat_e)
            se = flat_e[order]
            pos = jnp.arange(Tn * K) - jnp.searchsorted(se, se, side='left')
            tok = order // K
            valid = pos < CAP
            slot = jnp.where(valid, pos, CAP)
            buf = jnp.zeros((E, CAP + 1, H), x.dtype).at[se, slot].set(x[tok])[:, :CAP]
            h = jax.nn.silu(jnp.einsum('ech,ehf->ecf', buf, w_gate)) * jnp.einsum('ech,ehf->ecf', buf, w_up)
            out = jnp.einsum('ecf,efh->ech', h, w_down)
            gathered = out[se, jnp.minimum(pos, CAP - 1)] * valid.astype(x.dtype)[:, None]
            w = topk_w.reshape(-1)[order].astype(x.dtype)[:, None]
            return jax.ops.segment_sum(gathered * w, tok, num_segments=Tn)
        orig_shape = hidden_states.shape
        x = hidden_states.reshape(-1, H)
        router_logits = x @ gate_w
        topk_w, topk_ids = _grouped_topk(router_logits, bias)
        y = _routed_moe(x, topk_w, topk_ids, w_gate, w_up, w_down)
        shared = jax.nn.silu(x @ ws_gate) * (x @ ws_up) @ ws_down
        return (y + shared).reshape(orig_shape)
    x = L0_attn_x
    x = x + _layernorm(_L0_attn_ref(_layernorm(x, axis=-1), L0_attn_Wq, L0_attn_Wk, L0_attn_Wv, L0_attn_Wo), axis=-1)
    x = x + _layernorm(_L0_ffn_ref(_layernorm(x, axis=-1), L0_ffn_gate_w, L0_ffn_bias, L0_ffn_w_gate, L0_ffn_w_up, L0_ffn_w_down, L0_ffn_ws_gate, L0_ffn_ws_up, L0_ffn_ws_down), axis=-1)
    return x

_drawn_inputs = setup_inputs


def setup_inputs(seed=0):
    import zlib

    import numpy as np

    out = dict(_drawn_inputs(seed))
    spreads = {}
    factors = {}
    for name, (base, spread) in spreads.items():
        noise = np.random.default_rng([zlib.crc32(name.encode()), seed]).standard_normal(out[name].shape)
        drawn = base * np.exp(spread * noise) if base else spread * noise
        out[name] = jnp.asarray(drawn.astype(out[name].dtype))
    for name, factor in factors.items():
        out[name] = (out[name] * factor).astype(out[name].dtype)
    return out
```

```python
from contextlib import ExitStack

import numpy as np

import concourse.bass as bass
from concourse import mybir

F32 = mybir.dt.float32
F32R = mybir.dt.float32r
BF16 = mybir.dt.bfloat16
I32 = mybir.dt.int32
ALU = mybir.AluOpType
ACT = mybir.ActivationFunctionType
AX = mybir.AxisListType

P = 128
B, SEQ, HID = 4, 1024, 256
HEADS, KV_HEADS, HD = 16, 4, 128
GROUP = HEADS // KV_HEADS
NT = SEQ // P
NC = HID // P
EPS = 1e-5
NEG = -1e30

WA = NC * 4 * HD
WB = NC * 2 * HD
WO = GROUP * HID
WPACK = WA + WB + WO

STEPS = GROUP * NT
BODY = 2 * STEPS
TURNS = B * KV_HEADS // 2
ROT = 16
UNITS_BEFORE = [0, 1, 2, 3, 4, 6, 8, 10]
UNITS = 12


def prepare(nc, x, wpack, consts, w_split, xT_split, rows, sums):
    with ExitStack() as ctx:
        def sb(name, shape, dt=F32):
            return ctx.enter_context(nc.sbuf_tensor(name, shape, dt))

        def sem(name):
            return ctx.enter_context(nc.semaphore(name))

        ident = sb("pre_ident", [P, P])
        w_raw = sb("w_raw", [P, 2, WPACK])
        w_hl = sb("w_hl", [P, 2, 2, WPACK], F32R)
        x_raw = sb("x_raw", [P, 2, NT, HID])
        x_n = sb("x_n", [P, 2, NT, HID])
        stats = sb("pre_stats", [P, B, NT, 6])
        mv = sb("pre_mv", [P, B, NT, 2])
        var, std, rstd = (sb("pre_" + n, [P, B, NT]) for n in ("var", "std", "rstd"))
        xT = sb("pre_xT", [P, 2, 2, NC, SEQ], F32R)
        banks = [ctx.enter_context(nc.psum_tensor(f"pre_ps{i}", [P, 512], F32)) for i in range(2)]

        ident_in = sem("pre_ident_in")
        x_in = [sem(f"x_in{i}") for i in range(2)]
        w_in = [sem(f"w_in{i}") for i in range(2)]
        w_out = [sem(f"w_out{i}") for i in range(2)]
        xT_out = [sem(f"xT_out{i}") for i in range(2)]
        w_hi, w_lo = sem("w_hi"), sem("w_lo")
        stats_done, mv_done, xn_done = sem("pre_stats_done"), sem("pre_mv_done"), sem("xn_done")
        var_done, std_done, rstd_done = sem("pre_var_done"), sem("pre_std_done"), sem("pre_rstd_done")
        t_ready, t_hi, t_lo = sem("pre_t_ready"), sem("pre_t_hi"), sem("pre_t_lo")

        zeros = sb("pre_zeros", [P, NT * HID])
        zeroed, zeros_out = sem("pre_zeroed"), sem("zeros_out")

        block = ctx.enter_context(nc.Block())

        @block.gpsimd
        def _(pool):
            pool.memset(zeros[:], 0.0).then_inc(zeroed, 1)
            pool.wait_ge(zeroed, 1)
            pool.dma_start(rows[TOKENS:], zeros[0:TRASH, 0:HID + EXPERTS]).then_inc(zeros_out, 16)
            pool.dma_start(sums[0][TOKENS:], zeros[0:TRASH, 0:HID]).then_inc(zeros_out, 16)
            pool.dma_start(sums[1][TOKENS:], zeros[0:TRASH, 0:HID]).then_inc(zeros_out, 16)
            for b in range(B):
                pool.dma_start(sums[1][b * SEQ:(b + 1) * SEQ].rearrange("(p t) n -> p (t n)", p=P), zeros[:]).then_inc(zeros_out, 16)
            pool.wait_ge(zeros_out, 16 * (B + 3))

        units = [(c, half) for half in range(2) for c in range(NC)]

        @block.sync
        def _(sp):
            sp.dma_start(ident[:], consts["ident"]).then_inc(ident_in, 16)
            for b in range(B):
                if b >= 2:
                    sp.wait_ge(xn_done, NT * (b - 1))
                sp.dma_start(x_raw[:, b % 2], x[b].rearrange("(t p) n -> p t n", p=P)).then_inc(x_in[b % 2], 16)
                if b >= 2:
                    sp.wait_ge(w_lo, b - 1)
                sp.dma_start(w_raw[:, b % 2], wpack[b]).then_inc(w_in[b % 2], 16)
            for b in range(B):
                sp.wait_ge(t_lo, len(units) * (b + 1))
                sp.dma_start(xT_split[b], xT[:, b % 2].rearrange("p s c n -> p (s c n)").bitcast(F32)).then_inc(xT_out[b % 2], 16)
                sp.wait_ge(w_lo, b + 1)
                sp.dma_start(w_split[b], w_hl[:, b % 2].rearrange("p s n -> p (s n)").bitcast(F32)).then_inc(w_out[b % 2], 16)
            for i in range(2):
                sp.wait_ge(xT_out[i], 32)
                sp.wait_ge(w_out[i], 32)

        @block.vector
        def _(dve):
            for b in range(B):
                dve.wait_ge(x_in[b % 2], 16 * (b // 2 + 1))
                for t in range(NT):
                    dve.bn_stats(stats[:, b, t], x_raw[:, b % 2, t]).then_inc(stats_done, 1)
                dve.wait_ge(stats_done, NT * (b + 1))
                for t in range(NT):
                    dve.bn_aggr(mv[:, b, t], stats[:, b, t]).then_inc(mv_done, 1)
                dve.wait_ge(mv_done, NT * (b + 1))
                dve.tensor_scalar(var[:, b], mv[:, b, :, 1], EPS, None, ALU.add).then_inc(var_done, 1)
                dve.wait_ge(std_done, b + 1)
                dve.reciprocal(rstd[:, b], std[:, b]).then_inc(rstd_done, 1)
                dve.wait_ge(rstd_done, b + 1)
                if b >= 2:
                    dve.wait_ge(t_ready, len(units) * (b - 1))
                for t in range(NT):
                    dve.tensor_scalar(x_n[:, b % 2, t], x_raw[:, b % 2, t], mv[:, b, t, 0:1], rstd[:, b, t:t + 1],
                                      ALU.subtract, ALU.mult).then_inc(xn_done, 1)
                dve.wait_ge(w_hi, b + 1)
                if b >= 2:
                    dve.wait_ge(w_out[b % 2], 16)
                dve.tensor_tensor(w_hl[:, b % 2, 1], w_raw[:, b % 2], w_hl[:, b % 2, 0].bitcast(F32),
                                  ALU.subtract).then_inc(w_lo, 1)
                for u, (c, half) in enumerate(units):
                    dve.wait_ge(t_hi, len(units) * b + u + 1)
                    cols = slice(512 * half, 512 * half + 512)
                    dve.tensor_tensor(xT[:, b % 2, 1, c, cols], banks[u % 2][:],
                                      xT[:, b % 2, 0, c, cols].bitcast(F32), ALU.subtract).then_inc(t_lo, 1)

        @block.scalar
        def _(act):
            for b in range(B):
                act.wait_ge(var_done, b + 1)
                act.activation(std[:, b], var[:, b], ACT.Sqrt).then_inc(std_done, 1)
                act.wait_ge(w_in[b % 2], 16 * (b // 2 + 1))
                if b >= 2:
                    act.wait_ge(w_out[b % 2], 16)
                act.activation(w_hl[:, b % 2, 0], w_raw[:, b % 2], ACT.Copy).then_inc(w_hi, 1)
                for u, (c, half) in enumerate(units):
                    act.wait_ge(t_ready, len(units) * b + u + 1)
                    if b >= 2 and u == 0:
                        act.wait_ge(xT_out[b % 2], 16)
                    act.activation(xT[:, b % 2, 0, c, 512 * half:512 * half + 512], banks[u % 2][:],
                                   ACT.Copy).then_inc(t_hi, 1)

        @block.tensor
        def _(pe):
            pe.wait_ge(ident_in, 16)
            for b in range(B):
                for u, (c, half) in enumerate(units):
                    n = len(units) * b + u
                    pe.wait_ge(xn_done, NT * b + 4 * half + 4)
                    if n >= 2:
                        pe.wait_ge(t_lo, n - 1)
                    for i in range(4):
                        last = pe.transpose(banks[u % 2][:, i * P:(i + 1) * P],
                                            x_n[:, b % 2, 4 * half + i, c * P:(c + 1) * P], ident[:])
                    last.then_inc(t_ready, 1)


def attention(nc, consts, w_split, xT_split, y_parts):
    with ExitStack() as ctx:
        def sb(name, shape, dt=F32):
            return ctx.enter_context(nc.sbuf_tensor(name, shape, dt))

        def sem(name):
            return ctx.enter_context(nc.semaphore(name))

        ident = sb("ident", [P, P])
        ident_bf = sb("ident_bf", [P, P], BF16)
        mask_bf = sb("mask_bf", [P, P], BF16)
        cos_t = sb("cos_t", [P, NT, HD])
        sin_t = sb("sin_t", [P, NT, HD])
        xT = sb("xT", [P, 2, NC, SEQ], F32R)
        w_a = sb("w_a", [P, 2, NC, 4 * HD], F32R)
        w_b = sb("w_b", [P, 2, NC, 2 * HD], F32R)
        w_o = sb("w_o", [P, 2, 2, GROUP, HID], F32R)
        qT = sb("qT", [P, 2, 2, 2, SEQ], F32R)
        kT = sb("kT", [P, 2, 2, SEQ], F32R)
        v = sb("v", [P, 2, 2, NT, HD], F32R)
        probs = sb("probs", [P, 4, SEQ])
        pT = sb("pT", [P, 2, 2, NT, 2 * P], F32R)
        avT = sb("avT", [P, 2, 2 * P], F32R)
        y = sb("y", [P, NT, HID])
        y_part = sb("y_part", [P, 2, 2, HID])
        rope_c = sb("rope_c", [P, 512])
        rope_s = sb("rope_s", [P, 512])
        roped = sb("roped", [P, 512])
        neg_max = sb("neg_max", [P, 16])
        row_sum = sb("row_sum", [P, 16])
        inv_sum = sb("inv_sum", [P, 16])

        s_ps = ctx.enter_context(nc.psum_tensor("s_ps", [P, 2, SEQ], F32))
        t_ps = [ctx.enter_context(nc.psum_tensor(f"t_ps{i}", [P, 512], F32)) for i in range(2)]
        av_ps = ctx.enter_context(nc.psum_tensor("av_ps", [P, 512], F32))
        prod_ps = ctx.enter_context(nc.psum_tensor("prod_ps", [P, 512], F32))

        consts_in, bf_done = sem("consts_in"), sem("bf_done")
        xT_in, xT_landed, wa_in, wb_in = sem("xT_in"), sem("xT_landed"), sem("wa_in"), sem("wb_in")
        wo_in = [sem(f"wo_in{i}") for i in range(2)]
        wa_used, wb_used, wo_used = sem("wa_used"), sem("wb_used"), sem("wo_used")
        qkv_ready = sem("qkv_ready")
        bank_read = sem("bank_read")
        rope_added = sem("rope_added")
        qk_ready = sem("qk_ready")
        qk_hi, qk_lo = sem("qk_hi"), sem("qk_lo")
        v_hi = sem("v_hi")
        scores_ready, max_ready, exp_done = sem("scores_ready"), sem("max_ready"), sem("exp_done")
        pT_ready, pT_hi, pT_lo = sem("pT_ready"), sem("pT_hi"), sem("pT_lo")
        av_ready, av_hi, av_lo = sem("av_ready"), sem("av_hi"), sem("av_lo")
        inv_ready, op_ready, part_done, y_done = sem("inv_ready"), sem("op_ready"), sem("part_done"), sem("y_done")
        y_free = sem("y_free")
        y_out = [sem(f"y_out{i}") for i in range(4)]

        block = ctx.enter_context(nc.Block())

        def wait(eng, semaphore, turn, per_turn, at_least):
            if isinstance(turn, int):
                if per_turn * turn + at_least > 0:
                    eng.wait_ge(semaphore, per_turn * turn + at_least)
            else:
                assert at_least >= 0, (semaphore, at_least)
                eng.wait_ge(semaphore, turn * per_turn + max(at_least, 1))

        def tile(k):
            return k % NT

        def units_before(k):
            return (k // NT) * UNITS + UNITS_BEFORE[k % NT]

        def step_units(k):
            blocks = tile(k) + 1
            return [(units_before(k) + u, 4 * u, min(4, blocks - 4 * u)) for u in range((blocks + 3) // 4)]

        AT = {0: ("this", 8), 3: ("this", 9), 6: ("this", 10), 8: ("this", 11),
              11: ("next", 0), 14: ("next", 1), 16: ("next", 2), 19: ("next", 3),
              22: ("next", 4), 24: ("next", 5), 27: ("next", 6), 30: ("next", 7)}

        def produced_at(k):
            if k < 0 or k % STEPS not in AT:
                return None
            when, unit = AT[k % STEPS]
            return k // STEPS + (when == "next"), unit

        def program(eng, slot):
            for k in range(-1, ROT):
                slot(k, 0, False)
            with eng.Fori(0, TURNS - 1) as turn:
                for k in range(ROT, ROT + BODY):
                    slot(k, turn, False)
            for k in range(ROT, BODY + 4):
                slot(k, TURNS - 1, True)

        def exists(k, turn, last):
            return k >= 0 and not (last and k >= BODY)

        def made(group, last):
            return not (last and group >= 2)

        def destination(group, unit):
            cols = slice(256 * (unit % 4), 256 * (unit % 4) + 256)
            if unit < 4:
                return kT[:, group % 2, 0, cols], kT[:, group % 2, 1, cols], prod_ps[:, 0:256]
            pair = (unit - 4) // 4
            return (qT[:, pair, 0, :, cols], qT[:, pair, 1, :, cols],
                    prod_ps[:].rearrange("p (h n) -> p h n", h=2))

        @block.sync
        def _(sp):
            for dst, name in ((ident, "ident"), (cos_t, "cos"), (sin_t, "sin")):
                sp.dma_start(dst[:], consts[name]).then_inc(consts_in, 16)
            sp.dma_start(ident_bf[:], consts["ident_bf"]).then_inc(consts_in, 16)
            sp.dma_start(mask_bf[:], consts["mask_bf"]).then_inc(consts_in, 16)
            with sp.Fori(0, B) as b:
                sp.wait_ge(qkv_ready, b * (4 * UNITS))
                sp.dma_start(xT[:].rearrange("p s c n -> p (s c n)").bitcast(F32), xT_split[b]).then_inc(xT_in, 16)
                sp.wait_ge(xT_in, b * 16 + 16)
                sp.sem_inc(xT_landed, 1)
                for g in range(KV_HEADS):
                    src = w_split[g].rearrange("p (s n) -> p s n", s=2)
                    sp.wait_ge(wa_used, b * 4 + g)
                    sp.dma_start(w_a[:].rearrange("p s c n -> p s (c n)").bitcast(F32), src[:, :, 0:WA]).then_inc(wa_in, 16)
                    sp.wait_ge(wb_used, b * 4 + g)
                    sp.dma_start(w_b[:].rearrange("p s c n -> p s (c n)").bitcast(F32), src[:, :, WA:WA + WB]).then_inc(wb_in, 16)
                    if g < 2:
                        sp.wait_ge(wo_used, b * 4 + g - 1 if g else b * 4)
                    else:
                        sp.wait_ge(wo_used, b * 4 + g - 1)
                    sp.dma_start(w_o[:, g % 2].rearrange("p s h n -> p s (h n)").bitcast(F32),
                                 src[:, :, WA + WB:WPACK]).then_inc(wo_in[g % 2], 16)

        @block.tensor
        def _(pe):
            pe.wait_ge(consts_in, 5 * 16)

            def project(group, unit, turn):
                wait(pe, qk_lo, turn, 2 * UNITS, UNITS * group + unit)
                if unit in (0, 4):
                    wait(pe, wa_in, turn, 32, 16 * (group + 1))
                if unit == 8:
                    wait(pe, wb_in, turn, 32, 16 * (group + 1))
                w = w_b if unit >= 8 else w_a
                cols = slice(2 * HD, 4 * HD) if 4 <= unit < 8 else slice(0, 2 * HD)
                for i in range(2):
                    rows = slice((2 * (unit % 4) + i) * P, (2 * (unit % 4) + i + 1) * P)
                    passes = [(c, a, s) for c in range(NC) for a, s in ((0, 0), (0, 1), (1, 0))]
                    for n, (c, a, s) in enumerate(passes):
                        last = pe.matmul(prod_ps[:, i * 256:(i + 1) * 256], xT[:, a, c, rows], w[:, s, c, cols],
                                         start=(n == 0), stop=(n == len(passes) - 1))
                last.then_inc(qkv_ready, 1)

            def project_done(unit):
                if unit == 7:
                    pe.sem_inc(wa_used, 1)
                if unit == 11:
                    pe.sem_inc(wb_used, 1)

            def transpose_unit(group, unit, turn):
                wait(pe, rope_added, turn, 2 * UNITS, UNITS * group + unit + 1)
                heads = 1 if unit < 4 else 2
                for h in range(heads):
                    for i in range(2):
                        src = roped[:, i * heads * HD + h * HD:i * heads * HD + (h + 1) * HD]
                        last = pe.transpose(prod_ps[:, h * 256 + i * P:h * 256 + (i + 1) * P], src, ident[:])
                last.then_inc(qk_ready, 1)

            def scores(k, turn):
                group, h, i = k // STEPS, (k % STEPS) // NT, tile(k)
                wait(pe, exp_done, turn, BODY, k - 1)
                if h % 2 == 0 and i % 2 == 0:
                    wait(pe, qk_lo, turn, 2 * UNITS, UNITS * group + 4 + 4 * (h // 2) + i // 2 + 1)
                rows = slice(i * P, (i + 1) * P)
                width = (i + 1) * P
                for lo in range(0, width, 512):
                    hi = min(width, lo + 512)
                    out = s_ps[:, k % 2, lo:hi]
                    for n, (a, s) in enumerate(((0, 0), (0, 1), (1, 0))):
                        if n == 2 and hi == width:
                            pe.matmul(s_ps[:, k % 2, width - P:width], ident_bf[:], mask_bf[:], start=False, stop=False)
                        last = pe.matmul(out, qT[:, h // 2, a, h % 2, rows], kT[:, group % 2, s, lo:hi],
                                         start=(n == 0), stop=(n == 2))
                last.then_inc(scores_ready, 1)

            def transpose_probs(k, turn):
                wait(pe, exp_done, turn, BODY, k + 1)
                for n, first, count in step_units(k):
                    wait(pe, pT_lo, turn, BODY // NT * UNITS, n - 1)
                    for j in range(count):
                        last = pe.transpose(t_ps[n % 2][:, j * P:(j + 1) * P],
                                            probs[:, k % 4, (first + j) * P:(first + j + 1) * P], ident[:])
                    last.then_inc(pT_ready, 1)

            def attend(n, turn):
                group, p = n // 16, n % 4
                wait(pe, pT_lo, turn, BODY // NT * UNITS, units_before(2 * n + 2))
                wait(pe, part_done, turn, 32, n)
                for j in range(2 * p + 2):
                    cols = slice(P if j == 2 * p + 1 else 0, 2 * P)
                    for m, (a, s) in enumerate(((0, 0), (0, 1), (1, 0))):
                        last = pe.matmul(av_ps[:, cols], v[:, group % 2, a, j], pT[:, n % 2, s, j, cols],
                                         start=(j == 0 and m == 0), stop=(j == 2 * p + 1 and m == 2),
                                         skip_group_check=True)
                last.then_inc(av_ready, 1)

            def output(n, turn):
                group, h = n // 16, (n % 16) // 4
                wait(pe, av_lo, turn, 32, n + 1)
                if n % 16 == 0:
                    wait(pe, wo_in[group % 2], turn, 16, 16 * (group // 2 + 1))
                for i in range(2):
                    for m, (a, s) in enumerate(((0, 0), (0, 1), (1, 0))):
                        last = pe.matmul(av_ps[:, i * HID:(i + 1) * HID], avT[:, a, i * P:(i + 1) * P],
                                         w_o[:, group % 2, s, h], start=(m == 0), stop=(m == 2))
                last.then_inc(op_ready, 1)
                if n % 16 == 15:
                    pe.wait_ge(op_ready, turn * 32 + n + 1)
                    pe.sem_inc(wo_used, 1)

            def slot(k, turn, last):
                if exists(k + 1, turn, last):
                    scores(k + 1, turn)
                now, before = produced_at(k), produced_at(k - 2)
                if before and made(before[0], last):
                    transpose_unit(*before, turn)
                if exists(k - 1, turn, last):
                    transpose_probs(k - 1, turn)
                if k % 2 and k >= 3 and exists(k - 3, turn, last):
                    attend((k - 3) // 2, turn)
                if k % 2 == 0 and k >= 4 and exists(k - 4, turn, last):
                    output((k - 4) // 2, turn)
                if now and made(now[0], last):
                    project(*now, turn)
                    if now[1] in (7, 11):
                        wait(pe, qkv_ready, turn, 2 * UNITS, UNITS * now[0] + now[1] + 1)
                        project_done(now[1])

            for unit in range(8):
                project(0, unit, 0)
                if unit == 7:
                    pe.wait_ge(qkv_ready, 8)
                    project_done(7)
                transpose_unit(0, unit, 0)
            program(pe, slot)

        @block.vector
        def _(dve):
            dve.wait_ge(consts_in, 5 * 16)

            def rope(group, unit, turn):
                n = UNITS * group + unit
                j = unit % 4
                wait(dve, qkv_ready, turn, 2 * UNITS, n + 1)
                wait(dve, rope_added, turn, 2 * UNITS, n)
                if unit < 4:
                    src = prod_ps[:].rearrange("p (t n) -> p t n", t=2)
                    for out, table in ((rope_c, cos_t), (rope_s, sin_t)):
                        dve.tensor_tensor(out[:, 0:256].rearrange("p (t n) -> p t n", t=2), src[:, :, 0:HD],
                                          table[:, 2 * j:2 * j + 2], ALU.mult)
                    wait(dve, av_ready, turn, 32, 16 * (group - 1))
                    hi, lo = (v[:, group % 2, s, 2 * j:2 * j + 2] for s in range(2))
                    dve.tensor_copy(hi, src[:, :, HD:2 * HD]).then_inc(v_hi, 1)
                    wait(dve, v_hi, turn, 8, 4 * group + j + 1)
                    dve.tensor_tensor(lo, src[:, :, HD:2 * HD], hi.bitcast(F32), ALU.subtract).then_inc(bank_read, 1)
                else:
                    src = prod_ps[:].rearrange("p (t h n) -> p t h n", t=2, h=2)
                    for out, table in ((rope_c, cos_t), (rope_s, sin_t)):
                        tab = table[:, 2 * j:2 * j + 2].unsqueeze(2).broadcast_to([P, 2, 2, HD])
                        last = dve.tensor_tensor(out[:].rearrange("p (t h n) -> p t h n", t=2, h=2), src, tab, ALU.mult)
                    last.then_inc(bank_read, 1)

            def qk_low(group, unit, turn):
                wait(dve, qk_hi, turn, 2 * UNITS, UNITS * group + unit + 1)
                hi, lo, src = destination(group, unit)
                dve.tensor_tensor(lo, src, hi.bitcast(F32), ALU.subtract).then_inc(qk_lo, 1)

            def row_max(k, turn):
                wait(dve, scores_ready, turn, BODY, k + 1)
                dve.reduce_max(neg_max[:, k % 16:k % 16 + 1], s_ps[:, k % 2, 0:(tile(k) + 1) * P], AX.X,
                               negate=True).then_inc(max_ready, 1)

            def probs_low(k, turn):
                for n, first, count in step_units(k):
                    wait(dve, pT_hi, turn, BODY // NT * UNITS, n + 1)
                    hi, lo = (pT[:, (k // 2) % 2, s, first:first + count, (k % 2) * P:(k % 2 + 1) * P] for s in range(2))
                    dve.tensor_tensor(lo, t_ps[n % 2][:, 0:count * P].rearrange("p (j n) -> p j n", n=P),
                                      hi.bitcast(F32), ALU.subtract).then_inc(pT_lo, 1)

            def attended_low(n, turn):
                at = (2 * n) % 16
                wait(dve, exp_done, turn, BODY, 2 * n + 2)
                dve.reciprocal(inv_sum[:, at:at + 2], row_sum[:, at:at + 2]).then_inc(inv_ready, 1)
                wait(dve, av_hi, turn, 32, n + 1)
                dve.tensor_tensor(avT[:, 1], av_ps[:, 0:2 * P], avT[:, 0].bitcast(F32), ALU.subtract).then_inc(av_lo, 1)

            def slot(k, turn, last):
                if exists(k + 1, turn, last):
                    row_max(k + 1, turn)
                now, before = produced_at(k), produced_at(k - 2)
                if before and made(before[0], last):
                    qk_low(*before, turn)
                if exists(k - 1, turn, last):
                    probs_low(k - 1, turn)
                if k % 2 and k >= 3 and exists(k - 3, turn, last):
                    attended_low((k - 3) // 2, turn)
                if now and made(now[0], last):
                    rope(*now, turn)

            for unit in range(8):
                rope(0, unit, 0)
                qk_low(0, unit, 0)
            program(dve, slot)

        @block.scalar
        def _(act):
            def qk_high(group, unit, turn):
                wait(act, qk_ready, turn, 2 * UNITS, UNITS * group + unit + 1)
                if unit < 4:
                    wait(act, scores_ready, turn, BODY, STEPS * (group - 1))
                elif unit < 8:
                    wait(act, scores_ready, turn, BODY, STEPS * (group - 1) + 2 * NT)
                else:
                    wait(act, scores_ready, turn, BODY, STEPS * group)
                hi, _, src = destination(group, unit)
                act.activation(hi, src, ACT.Copy).then_inc(qk_hi, 1)

            def exponentials(k, turn):
                width = (tile(k) + 1) * P
                wait(act, max_ready, turn, BODY, k + 1)
                wait(act, pT_ready, turn, BODY // NT * UNITS, units_before(k - 3))
                wait(act, inv_ready, turn, 32, k // 2 - 7)
                act.activation(probs[:, k % 4, 0:width], s_ps[:, k % 2, 0:width], ACT.Exp,
                               bias=neg_max[:, k % 16:k % 16 + 1],
                               accum_out=row_sum[:, k % 16:k % 16 + 1]).then_inc(exp_done, 1)

            def probs_high(k, turn):
                for n, first, count in step_units(k):
                    wait(act, pT_ready, turn, BODY // NT * UNITS, n + 1)
                    wait(act, av_ready, turn, 32, k // 2 - 1)
                    act.activation(pT[:, (k // 2) % 2, 0, first:first + count, (k % 2) * P:(k % 2 + 1) * P],
                                   t_ps[n % 2][:, 0:count * P].rearrange("p (j n) -> p j n", n=P),
                                   ACT.Copy).then_inc(pT_hi, 1)

            def attended_high(n, turn):
                wait(act, av_ready, turn, 32, n + 1)
                wait(act, op_ready, turn, 32, n)
                act.activation(avT[:, 0], av_ps[:, 0:2 * P], ACT.Copy).then_inc(av_hi, 1)

            def output_scaled(n, turn):
                wait(act, op_ready, turn, 32, n + 1)
                wait(act, inv_ready, turn, 32, n + 1)
                wait(act, y_done, turn, 32, n - 1)
                for i in range(2):
                    at = (2 * n + i) % 16
                    last = act.activation(y_part[:, n % 2, i], av_ps[:, i * HID:(i + 1) * HID], ACT.Copy,
                                          scale=inv_sum[:, at:at + 1])
                last.then_inc(part_done, 1)

            def slot(k, turn, last):
                before = produced_at(k - 2)
                if before and made(before[0], last):
                    qk_high(*before, turn)
                if exists(k - 1, turn, last):
                    probs_high(k - 1, turn)
                if exists(k + 1, turn, last):
                    exponentials(k + 1, turn)
                if k % 2 and k >= 3 and exists(k - 3, turn, last):
                    attended_high((k - 3) // 2, turn)
                if k % 2 == 0 and k >= 4 and exists(k - 4, turn, last):
                    output_scaled((k - 4) // 2, turn)

            for unit in range(8):
                qk_high(0, unit, 0)
            program(act, slot)

        @block.gpsimd
        def _(pool):
            def rope_add(group, unit, turn):
                n = UNITS * group + unit
                wait(pool, bank_read, turn, 2 * UNITS, n + 1)
                wait(pool, qk_ready, turn, 2 * UNITS, n)
                width = 256 if unit < 4 else 512
                out, c, s = (a[:, 0:width].rearrange("p (m n) -> p m n", n=HD) for a in (roped, rope_c, rope_s))
                half = HD // 2
                pool.tensor_tensor(out[:, :, 0:half], c[:, :, 0:half], s[:, :, half:HD], ALU.add)
                pool.tensor_tensor(out[:, :, half:HD], c[:, :, half:HD], s[:, :, 0:half], ALU.add).then_inc(rope_added, 1)

            def add_output(n, turn):
                p = n % 4
                out = y[:, 2 * p:2 * p + 2]
                wait(pool, part_done, turn, 32, n + 1)
                if n % 32 < 4:
                    wait(pool, y_out[p], turn, 16, 16 * (n // 32))
                    pool.sem_inc(y_free, 1)
                    pool.tensor_copy(out, y_part[:, n % 2]).then_inc(y_done, 1)
                else:
                    wait(pool, y_done, turn, 32, n - 3)
                    pool.tensor_tensor(out, out, y_part[:, n % 2], ALU.add).then_inc(y_done, 1)

            def store(n, turn):
                p = n % 4
                wait(pool, y_done, turn, 32, n + 1)
                pool.dma_start(y_parts[turn + n // 32, :, 2 * p:2 * p + 2], y[:, 2 * p:2 * p + 2]).then_inc(y_out[p], 16)

            def slot(k, turn, last):
                now = produced_at(k)
                if now and made(now[0], last):
                    rope_add(*now, turn)
                if k % 2 == 0 and k >= 4 and exists(k - 4, turn, last):
                    add_output((k - 4) // 2, turn)
                    if ((k - 4) // 2) % 32 >= 28:
                        store((k - 4) // 2, turn)

            for unit in range(8):
                rope_add(0, unit, 0)
            program(pool, slot)
            for p in range(4):
                pool.wait_ge(y_out[p], 16 * TURNS)




TRASH = 48
EXPERTS, TOP, FF = 64, 6, 96
GROUPS_R, TOP_GROUPS = 8, 4
SLOTS = 48
SCALE = 2.5
TOKENS = B * SEQ
BLOCKS = EXPERTS * SLOTS // P
ROW = HID + EXPERTS
RSQRT_STEPS = 4
LINKS = 74


class Links:

    def __init__(self, eng, semaphore, turn, per_turn):
        self.eng, self.semaphore, self.turn, self.per_turn, self.n = eng, semaphore, turn, per_turn, 0

    def __call__(self, instruction):
        instruction.then_inc(self.semaphore, 1)
        self.n += 1
        self.eng.wait_ge(self.semaphore, self.turn * self.per_turn + self.n)


def layer_norm(dve, link, out, src, tmp, settled):
    stats, mv, var, guess, a = tmp
    tiles = src.shape[1]
    for t in range(tiles):
        last = dve.bn_stats(stats[:, t], src[:, t])
    link(last)
    settled()
    for t in range(tiles):
        last = dve.bn_aggr(mv[:, t], stats[:, t])
    link(last)
    link(dve.tensor_scalar(var[:], mv[:, :, 1], EPS, None, ALU.add))
    link(dve.tensor_scalar(guess[:].bitcast(I32), var[:].bitcast(I32), 1, None, ALU.arith_shift_right))
    link(dve.tensor_scalar(guess[:].bitcast(I32), guess[:].bitcast(I32), -1.0, float(0x5F3759DF), ALU.mult, ALU.add))
    for _ in range(RSQRT_STEPS):
        link(dve.tensor_tensor(a[:], guess[:], guess[:], ALU.mult))
        link(dve.tensor_tensor(a[:], a[:], var[:], ALU.mult))
        link(dve.tensor_scalar(a[:], a[:], -0.5, 1.5, ALU.mult, ALU.add))
        link(dve.tensor_tensor(guess[:], guess[:], a[:], ALU.mult))
    for t in range(tiles):
        last = dve.tensor_scalar(out[:, t], src[:, t], mv[:, t, 0:1], guess[:, t:t + 1], ALU.subtract, ALU.mult)
    link(last)


def route(nc, x, y_parts, consts, x1_rows, rows, y_rows, slot_info):
    with ExitStack() as ctx:
        def sb(name, shape, dt=F32):
            return ctx.enter_context(nc.sbuf_tensor("r_" + name, shape, dt))

        def sem(name):
            return ctx.enter_context(nc.semaphore("r_" + name))

        def psum(name):
            return ctx.enter_context(nc.psum_tensor("r_" + name, [P, 512], F32))

        ident = sb("ident", [P, P])
        gate_w = sb("gate_w", [P, NC, EXPERTS])
        bias = sb("bias", [P, EXPERTS])
        lower = sb("lower", [P, GROUPS_R * GROUPS_R])
        tri = sb("tri", [P, P], BF16)
        ones = sb("ones", [P, P], BF16)
        token = sb("token", [P, B * NT * 4], BF16)
        zeros = sb("zeros", [P, BLOCKS * 3], BF16)
        slot_c = sb("slot_c", [P, SLOTS, EXPERTS], BF16)
        ws_in = sb("ws_in", [P, 2, NC, FF])
        ws_down = sb("ws_down", [FF, HID])
        xb = sb("xb", [P, NT, HID])
        ya = sb("ya", [P, NT, HID])
        yb = sb("yb", [P, NT, HID])
        x1 = sb("x1", [P, NT, HID])
        row = sb("row", [P, NT, ROW])
        x2T = sb("x2T", [P, NC, SEQ])
        norm_tmp = (sb("stats", [P, NT, 6]), sb("mv", [P, NT, 2]), sb("var", [P, NT]), sb("guess", [P, NT]),
                    sb("newton", [P, NT]))
        th, score, biased, masked, replaced, selected, weight, taken = (
            sb(n, [P, NT, EXPERTS]) for n in ("th", "score", "biased", "masked", "replaced", "selected", "weight", "taken"))
        hi1, lo1 = sb("hi1", [P, NT * GROUPS_R, 4]), sb("lo1", [P, NT * GROUPS_R, 4])
        hi2, mid2, lo2 = (sb(n, [P, NT * GROUPS_R, 2]) for n in ("hi2", "mid2", "lo2"))
        hi3, mid3, lo3, group_score, group_rank = (sb(n, [P, NT * GROUPS_R]) for n in
                                                   ("hi3", "mid3", "lo3", "group_score", "group_rank"))
        at_least, above = (sb(n, [P, NT, GROUPS_R * GROUPS_R]) for n in ("at_least", "above"))
        top8 = sb("top8", [P, NT, 8])
        weight_sum, weight_inv = sb("weight_sum", [P, NT]), sb("weight_inv", [P, NT])
        selected_bf = sb("selected_bf", [P, NT, EXPERTS], BF16)
        before = sb("before", [P, EXPERTS])
        here = sb("here", [P, EXPERTS])
        before_bf = sb("before_bf", [P, EXPERTS], BF16)
        position = sb("position", [P, NT, EXPERTS], BF16)
        one_hot = sb("one_hot", [P, 2, SLOTS, EXPERTS], BF16)
        th_s, act_s = sb("th_s", [FF, SEQ]), sb("act_s", [FF, SEQ])
        h_s = sb("h_s", [FF, SEQ])
        y_s = sb("y_s", [P, NT, HID])
        info = sb("info", [P, BLOCKS, 3])

        t_ps = [psum("t_ps0"), psum("t_ps1")]
        logit_ps, count_ps, info_ps, gate_ps, up_ps, down_ps = (psum(n) for n in
                                                                ("logit", "count", "info_ps", "gate_ps", "up_ps", "down_ps"))

        consts_in = sem("consts_in")
        x_in, ya_in, yb_in, x1_out, row_out, y_out = (sem(n) for n in ("x_in", "ya_in", "yb_in", "x1_out", "row_out", "y_out"))
        chain = sem("chain")
        zeroed, waited = sem("zeroed"), sem("waited")
        x1_done, x2_done, row_done = sem("x1_done"), sem("x2_done"), sem("row_done")
        t_ready, t_read = sem("t_ready"), sem("t_read")
        logits_ready, tanh_done = sem("logits_ready"), sem("tanh_done")
        selected_done, count_ready, hot_done, hot_used = sem("selected_done"), sem("count_ready"), sem("hot_done"), sem("hot_used")
        gate_ready, up_ready, gate_tanh, h_done, down_ready, down_read = (
            sem(n) for n in ("gate_ready", "up_ready", "gate_tanh", "h_done", "down_ready", "down_read"))
        info_read, info_out = sem("info_read"), sem("info_out")

        block = ctx.enter_context(nc.Block())
        NCONST = 10
        HALVES = SEQ // 512

        @block.sync
        def _(sp):
            for dst, name in ((ident, "ident"), (gate_w, "gate_w"), (bias, "bias"), (lower, "lower"), (tri, "tri"),
                              (ones, "ones"), (token, "token"), (slot_c, "slot_c"), (ws_in, "ws_in"), (ws_down, "ws_down")):
                sp.dma_start(dst[:], consts[name]).then_inc(consts_in, 16)
            with sp.Fori(0, B) as b:
                sp.wait_ge(x1_done, b)
                sp.dma_start(ya[:], y_parts[b * 2]).then_inc(ya_in, 16)
                sp.dma_start(yb[:], y_parts[b * 2 + 1]).then_inc(yb_in, 16)
                sp.dma_start(xb[:], x[b].rearrange("(t p) n -> p t n", p=P)).then_inc(x_in, 16)
                sp.wait_ge(x1_done, b + 1)
                sp.dma_start(x1_rows[b], x1[:]).then_inc(x1_out, 16)
                sp.wait_ge(row_done, b + 1)
                sp.dma_start(rows[bass.ds(b * SEQ, SEQ), :].rearrange("(t p) n -> p t n", p=P), row[:]).then_inc(row_out, 16)
                sp.wait_ge(down_read, b * (NT // 2) + NT // 2)
                sp.dma_start(y_rows[bass.ds(b * SEQ, SEQ), :].rearrange("(t p) n -> p t n", p=P), y_s[:]).then_inc(y_out, 16)
            sp.wait_ge(info_read, 1)
            sp.dma_start(slot_info, info[:]).then_inc(info_out, 16)
            for s, n in ((x1_out, B), (row_out, B), (y_out, B), (info_out, 1)):
                sp.wait_ge(s, 16 * n)

        @block.vector
        def _(dve):
            PER = LINKS

            def settled():
                dve.sem_inc(waited, 1)

            dve.memset(zeros[:], 0.0)
            dve.memset(before[:], 0.0)
            dve.memset(before_bf[:], 0.0).then_inc(zeroed, 1)
            dve.wait_ge(consts_in, 16 * NCONST)
            dve.wait_ge(zeroed, 1)
            with dve.Fori(0, B) as b:
                link = Links(dve, chain, b, PER)
                dve.wait_ge(ya_in, b * 16 + 16)
                dve.wait_ge(yb_in, b * 16 + 16)
                dve.wait_ge(x1_out, b * 16)
                link(dve.tensor_tensor(ya[:], ya[:], yb[:], ALU.add))
                layer_norm(dve, link, ya, ya, norm_tmp, settled)
                dve.wait_ge(x_in, b * 16 + 16)
                dve.tensor_tensor(x1[:], ya[:], xb[:], ALU.add).then_inc(x1_done, 1)
                dve.wait_ge(x1_done, b + 1)
                dve.wait_ge(row_out, b * 16)
                layer_norm(dve, link, row[:, :, 0:HID], x1, norm_tmp, settled)
                dve.sem_inc(x2_done, 1)

                dve.wait_ge(tanh_done, b + 1)
                link(dve.tensor_scalar(score[:], th[:], 0.5, 0.5, ALU.mult, ALU.add))
                link(dve.tensor_tensor(biased[:], score[:], bias[:].unsqueeze(1).broadcast_to([P, NT, EXPERTS]), ALU.add))
                v8 = biased[:].rearrange("p t (g n) -> p (t g) n", g=GROUPS_R)
                dve.tensor_tensor(hi1[:], v8[:, :, 0:4], v8[:, :, 4:8], ALU.max)
                link(dve.tensor_tensor(lo1[:], v8[:, :, 0:4], v8[:, :, 4:8], ALU.min))
                dve.tensor_tensor(hi2[:], hi1[:, :, 0:2], hi1[:, :, 2:4], ALU.max)
                dve.tensor_tensor(mid2[:], hi1[:, :, 0:2], hi1[:, :, 2:4], ALU.min)
                link(dve.tensor_tensor(lo2[:], lo1[:, :, 0:2], lo1[:, :, 2:4], ALU.max))
                link(dve.tensor_tensor(lo2[:], lo2[:], mid2[:], ALU.max))
                dve.tensor_tensor(hi3[:], hi2[:, :, 0], hi2[:, :, 1], ALU.max)
                dve.tensor_tensor(mid3[:], hi2[:, :, 0], hi2[:, :, 1], ALU.min)
                link(dve.tensor_tensor(lo3[:], lo2[:, :, 0], lo2[:, :, 1], ALU.max))
                link(dve.tensor_tensor(lo3[:], lo3[:], mid3[:], ALU.max))
                link(dve.tensor_tensor(group_score[:], hi3[:], lo3[:], ALU.add))

                gs = group_score[:].rearrange("p (t g) -> p t g", t=NT)
                other = gs.unsqueeze(2).broadcast_to([P, NT, GROUPS_R, GROUPS_R])
                own = gs.unsqueeze(3).broadcast_to([P, NT, GROUPS_R, GROUPS_R])
                square = lambda a: a[:].rearrange("p t (g h) -> p t g h", g=GROUPS_R)
                dve.tensor_tensor(square(at_least), other, own, ALU.is_ge)
                link(dve.tensor_tensor(square(above), other, own, ALU.is_gt))
                link(dve.tensor_tensor(at_least[:], at_least[:], above[:], ALU.subtract))
                link(dve.tensor_tensor(at_least[:], at_least[:], lower[:].unsqueeze(1).broadcast_to([P, NT, 64]), ALU.mult))
                link(dve.tensor_tensor(at_least[:], at_least[:], above[:], ALU.add))
                link(dve.tensor_reduce(group_rank[:].rearrange("p (t g) -> p t g", t=NT), square(at_least), AX.X, ALU.add))
                link(dve.tensor_scalar(group_rank[:], group_rank[:], TOP_GROUPS - 0.5, NEG, ALU.is_gt, ALU.mult))
                link(dve.tensor_tensor(masked[:].rearrange("p t (g n) -> p (t g) n", g=GROUPS_R), v8,
                                       group_rank[:].unsqueeze(2).broadcast_to([P, NT * GROUPS_R, 8]), ALU.add))
                settled()
                for t in range(NT):
                    last = dve.max(top8[:, t], masked[:, t])
                link(last)
                link(dve.memset(top8[:, :, TOP:8], NEG))
                settled()
                for t in range(NT):
                    last = dve.match_replace(replaced[:, t], top8[:, t], masked[:, t], NEG)
                link(last)
                dve.wait_ge(count_ready, b)
                link(dve.tensor_tensor(selected[:], masked[:], replaced[:], ALU.not_equal))
                dve.tensor_copy(selected_bf[:], selected[:]).then_inc(selected_done, 1)
                link(dve.tensor_tensor(weight[:], score[:], selected[:], ALU.mult))
                link(dve.tensor_reduce(weight_sum[:], weight[:], AX.X, ALU.add))
                link(dve.reciprocal(weight_inv[:], weight_sum[:]))
                link(dve.tensor_scalar(weight_inv[:], weight_inv[:], SCALE, None, ALU.mult))
                dve.tensor_tensor(row[:, :, HID:ROW], weight[:], weight_inv[:].unsqueeze(2).broadcast_to([P, NT, EXPERTS]),
                                  ALU.mult).then_inc(row_done, 1)
                for half in range(HALVES):
                    cols = slice(512 * half, 512 * half + 512)
                    dve.wait_ge(gate_tanh, b * HALVES + half + 1)
                    link(dve.scalar_tensor_tensor(act_s[:, cols], th_s[:, cols], 1.0, gate_ps[0:FF], ALU.add, ALU.mult))
                    dve.wait_ge(up_ready, b * HALVES + half + 1)
                    dve.wait_ge(down_ready, b * (NT // 2))
                    dve.scalar_tensor_tensor(h_s[:, cols], act_s[:, cols], 0.5, up_ps[0:FF], ALU.mult, ALU.mult).then_inc(h_done, 1)
                link(dve.tensor_scalar(taken[:], selected[:], -4096.0, 4096.0, ALU.mult, ALU.add))
                dve.wait_ge(count_ready, b + 1)
                dve.wait_ge(hot_used, b * NT)
                dve.tensor_tensor(position[:], count_ps[:].rearrange("p (t e) -> p t e", t=NT), taken[:], ALU.add)
                link(dve.tensor_reduce(here[:], selected[:].rearrange("p t e -> p e t"), AX.X, ALU.add))
                link(dve.tensor_tensor(before[:], before[:], here[:], ALU.add))
                link(dve.tensor_copy(before_bf[:], before[:]))
                for t in range(NT):
                    if t >= 2:
                        dve.wait_ge(hot_used, b * NT + t - 1)
                    dve.tensor_tensor(one_hot[:, t % 2], slot_c[:], position[:, t].unsqueeze(1).broadcast_to([P, SLOTS, EXPERTS]),
                                      ALU.is_equal).then_inc(hot_done, 1)
                assert link.n == PER, link.n
            dve.wait_ge(hot_used, B * NT)
            dve.tensor_copy(info[:], info_ps[:, 0:BLOCKS * 3].rearrange("p (n k) -> p n k", k=3)).then_inc(info_read, 1)

        @block.scalar
        def _(act):
            with act.Fori(0, B) as b:
                for u in range(4):
                    c, half = u % 2, u // 2
                    act.wait_ge(t_ready, b * 4 + u + 1)
                    act.activation(x2T[:, c, 512 * half:512 * half + 512], t_ps[u % 2][:], ACT.Copy).then_inc(t_read, 1)
                act.wait_ge(logits_ready, b + 1)
                act.activation(th[:], logit_ps[:].rearrange("p (t e) -> p t e", t=NT), ACT.Tanh, scale=0.5).then_inc(tanh_done, 1)
                for half in range(HALVES):
                    act.wait_ge(gate_ready, b * HALVES + half + 1)
                    act.activation(th_s[:, 512 * half:512 * half + 512], gate_ps[0:FF], ACT.Tanh, scale=0.5).then_inc(gate_tanh, 1)
                act.wait_ge(y_out, b * 16)
                for u in range(NT // 2):
                    act.wait_ge(down_ready, b * (NT // 2) + u + 1)
                    act.activation(y_s[:, 2 * u:2 * u + 2], down_ps[:].rearrange("p (t n) -> p t n", t=2), ACT.Copy).then_inc(down_read, 1)

        @block.tensor
        def _(pe):
            pe.wait_ge(consts_in, 16 * NCONST)
            pe.wait_ge(zeroed, 1)
            pe.matmul(info_ps[:, 0:BLOCKS * 3], ones[:], zeros[:], start=True, stop=True)
            with pe.Fori(0, B) as b:
                pe.wait_ge(x2_done, b + 1)
                for u in range(4):
                    c, half = u % 2, u // 2
                    pe.wait_ge(t_read, b * 4 + max(u - 1, 0))
                    for i in range(4):
                        last = pe.transpose(t_ps[u % 2][:, i * P:(i + 1) * P], row[:, 4 * half + i, c * P:(c + 1) * P], ident[:])
                    last.then_inc(t_ready, 1)
                pe.wait_ge(t_read, b * 4 + 4)
                pe.wait_ge(tanh_done, b)
                for t in range(NT):
                    for c in range(NC):
                        last = pe.matmul(logit_ps[:, t * EXPERTS:(t + 1) * EXPERTS], x2T[:, c, t * P:(t + 1) * P], gate_w[:, c],
                                         start=(c == 0), stop=(c == NC - 1))
                last.then_inc(logits_ready, 1)
                for half in range(HALVES):
                    cols = slice(512 * half, 512 * half + 512)
                    pe.wait_ge(h_done, b * HALVES + half)
                    for k, (bank, ready) in enumerate(((gate_ps, gate_ready), (up_ps, up_ready))):
                        for c in range(NC):
                            last = pe.matmul(bank[0:FF], ws_in[:, k, c], x2T[:, c, cols], start=(c == 0), stop=(c == NC - 1))
                        last.then_inc(ready, 1)
                pe.wait_ge(selected_done, b + 1)
                pe.wait_ge(chain, b * LINKS)
                for t in range(NT):
                    out = count_ps[:, t * EXPERTS:(t + 1) * EXPERTS]
                    pe.matmul(out, tri[:], selected_bf[:, t], start=True, stop=False)
                    for i in range(t):
                        pe.matmul(out, ones[:], selected_bf[:, i], start=False, stop=False)
                    last = pe.matmul(out, ones[:], before_bf[:], start=False, stop=True)
                last.then_inc(count_ready, 1)
                for t in range(NT):
                    pe.wait_ge(hot_done, b * NT + t + 1)
                    for n in range(BLOCKS):
                        last = pe.matmul(info_ps[:, 3 * n:3 * n + 3], one_hot[:, t % 2, 2 * n:2 * n + 2].rearrange("p c e -> p (c e)"),
                                         token[:, bass.ds(b * (4 * NT) + 4 * t, 3)], start=False, stop=True, skip_group_check=True)
                    last.then_inc(hot_used, 1)
                for u in range(NT // 2):
                    pe.wait_ge(h_done, b * HALVES + u // 2 + 1)
                    pe.wait_ge(down_read, b * (NT // 2) + u)
                    for i in range(2):
                        t = 2 * u + i
                        last = pe.matmul(down_ps[:, i * HID:(i + 1) * HID], h_s[:, t * P:(t + 1) * P], ws_down[:], start=True, stop=True)
                    last.then_inc(down_ready, 1)


def experts(nc, consts, rows, slot_info, slot_rows, slot_weights, expert_w, sums):
    with ExitStack() as ctx:
        def sb(name, shape, dt=F32):
            return ctx.enter_context(nc.sbuf_tensor("e_" + name, shape, dt))

        def sem(name):
            return ctx.enter_context(nc.semaphore("e_" + name))

        def psum(name):
            return ctx.enter_context(nc.psum_tensor("e_" + name, [P, 512], F32))

        TURN = 8
        N_TURNS = EXPERTS // TURN
        PACK_IN, PACK = 2 * NC * FF, 2 * NC * FF + HID
        GATHERS = 6

        ident = sb("ident", [P, P])
        diag = sb("diag", [P, EXPERTS])
        trash = sb("trash", [P, BLOCKS])
        info = sb("info", [P, BLOCKS, 3])
        row_f, row_i = sb("row_f", [P, BLOCKS]), sb("row_i", [P, BLOCKS], I32)
        gathered = sb("gathered", [P, BLOCKS, ROW])
        own_w = sb("own_w", [P, BLOCKS, EXPERTS])
        w_slot = sb("w_slot", [P, BLOCKS])
        rows_by_slot, w_by_slot = sb("rows_by_slot", [BLOCKS, P], I32), sb("w_by_slot", [BLOCKS, P])
        by_slot_ready, by_slot_done = sem("by_slot_ready"), sem("by_slot_done")
        xsT = sb("xsT", [P, NC, EXPERTS, SLOTS])
        dest = sb("dest", [SLOTS, EXPERTS], I32)
        w_dest = sb("w_dest", [SLOTS, EXPERTS])
        w_in = sb("w_in", [P, 2, TURN, PACK_IN])
        w_down = sb("w_down", [FF, 2, TURN, HID])
        th, a, h = (sb(n, [FF, TURN * SLOTS]) for n in ("th", "a", "h"))
        y = sb("y", [SLOTS, 2, TURN, HID])

        t_ps = [psum("t_ps0"), psum("t_ps1")]
        gate_ps, up_ps = psum("gate"), psum("up")
        y_ps = [psum("y_ps0"), psum("y_ps1")]

        consts_in, chain = sem("consts_in"), sem("chain")
        row_ready, w_ready, slots_out, dest_in = sem("row_ready"), sem("w_ready"), sem("slots_out"), sem("dest_in")
        gathered_in = [sem(f"gathered_in{i}") for i in range(BLOCKS // GATHERS)]
        wi_in = [sem(f"wi_in{i}") for i in range(2)]
        wd_in = [sem(f"wd_in{i}") for i in range(2)]
        t_ready, t_read = sem("t_ready"), sem("t_read")
        gate_ready, up_ready, tanh_done, h_done, y_ready, y_read = (
            sem(n) for n in ("gate_ready", "up_ready", "tanh_done", "h_done", "y_ready", "y_read"))
        added = [sem(f"added{i}") for i in range(2)]

        block = ctx.enter_context(nc.Block())
        UNITS_T = 2 * BLOCKS // 4

        @block.sync
        def _(sp):
            for dst, src in ((ident, consts["ident"]), (diag, consts["diag"]), (trash, consts["trash"]), (info, slot_info)):
                sp.dma_start(dst[:], src).then_inc(consts_in, 16)

            def load(e, parity):
                w = expert_w[bass.ds(e, TURN)] if not isinstance(e, int) else expert_w[e:e + TURN]
                sp.dma_start(w_in[:, parity], w[:, :, 0:PACK_IN].rearrange("e p n -> p e n")).then_inc(wi_in[parity], 16)
                sp.dma_start(w_down[:, parity], w[:, 0:FF, PACK_IN:PACK].rearrange("e p n -> p e n")).then_inc(wd_in[parity], 16)

            load(0, 0)
            load(TURN, 1)
            sp.wait_ge(by_slot_done, 1)
            sp.dma_start(slot_rows.rearrange("(n p) -> n p", p=P), rows_by_slot[:]).then_inc(slots_out, 16)
            sp.wait_ge(by_slot_done, 2)
            sp.dma_start(slot_weights.rearrange("(n p) -> n p", p=P), w_by_slot[:]).then_inc(slots_out, 16)
            sp.wait_ge(slots_out, 32)
            sp.dma_start(dest[:], slot_rows.rearrange("(c e) -> c e", e=EXPERTS)).then_inc(dest_in, 16)
            sp.dma_start(w_dest[:], slot_weights.rearrange("(c e) -> c e", e=EXPERTS)).then_inc(dest_in, 16)
            with sp.Fori(0, N_TURNS // 2 - 1) as i:
                for parity in range(2):
                    sp.wait_ge(y_ready, i * TURN + (parity + 1) * (TURN // 2))
                    load(i * (2 * TURN) + (2 + parity) * TURN, parity)

        @block.gpsimd
        def _(pool):
            pool.wait_ge(row_ready, 1)
            for n in range(BLOCKS):
                pool.indirect_dma_start(gathered[:, n], None, rows, bass.IndirectOffsetOnAxis(row_i[:, n:n + 1], 0),
                                        bounds_check=TOKENS + TRASH - 1, oob_is_err=False).then_inc(gathered_in[n // GATHERS], 16)
            pool.wait_ge(dest_in, 32)
            for e in range(EXPERTS):
                if e % 2 == 0:
                    pool.wait_ge(y_read, e // 2 + 1)
                if e >= 2:
                    pool.wait_ge(added[e % 2], 16 * (e // 2))
                pool.indirect_dma_start(sums[e % 2], bass.IndirectOffsetOnAxis(dest[:, e:e + 1], 0), y[:, (e // TURN) % 2, e % TURN], None,
                                        bounds_check=TOKENS + TRASH - 1, compute_op=ALU.add).then_inc(added[e % 2], 16)
            for i in range(2):
                pool.wait_ge(added[i], 16 * EXPERTS // 2)

        @block.vector
        def _(dve):
            link = Links(dve, chain, 0, 0)
            dve.wait_ge(consts_in, 4 * 16)
            link(dve.scalar_tensor_tensor(row_f[:], info[:, :, 1], float(P), info[:, :, 0], ALU.mult, ALU.add))
            link(dve.tensor_tensor(row_f[:], row_f[:], trash[:], ALU.subtract))
            link(dve.tensor_tensor(row_f[:], row_f[:], info[:, :, 2], ALU.mult))
            link(dve.tensor_tensor(row_f[:], row_f[:], trash[:], ALU.add))
            dve.tensor_copy(row_i[:], row_f[:]).then_inc(row_ready, 1)
            dve.wait_ge(by_slot_ready, 1)
            dve.tensor_copy(rows_by_slot[:], gate_ps[0:BLOCKS, 0:P]).then_inc(by_slot_done, 1)
            for g in range(BLOCKS // GATHERS):
                dve.wait_ge(gathered_in[g], 16 * GATHERS)
            link(dve.tensor_tensor(own_w[:], gathered[:, :, HID:ROW], diag[:].unsqueeze(1).broadcast_to([P, BLOCKS, EXPERTS]), ALU.mult))
            dve.tensor_reduce(w_slot[:], own_w[:], AX.X, ALU.add).then_inc(w_ready, 1)
            dve.wait_ge(by_slot_ready, 2)
            dve.tensor_copy(w_by_slot[:], up_ps[0:BLOCKS, 0:P]).then_inc(by_slot_done, 1)
            with dve.Fori(0, N_TURNS) as i:
                dve.wait_ge(tanh_done, i + 1)
                dve.scalar_tensor_tensor(a[:], th[:], 1.0, gate_ps[0:FF, 0:TURN * SLOTS], ALU.add, ALU.mult).then_inc(chain, 1)
                dve.wait_ge(chain, i + 6)
                dve.wait_ge(up_ready, i + 1)
                dve.wait_ge(y_ready, i * (TURN // 2))
                dve.scalar_tensor_tensor(h[:], a[:], 0.5, up_ps[0:FF, 0:TURN * SLOTS], ALU.mult, ALU.mult).then_inc(h_done, 1)

        @block.scalar
        def _(act):
            for u in range(UNITS_T):
                act.wait_ge(t_ready, u + 1)
                c, n = u % 2, 4 * (u // 2)
                act.activation(xsT[:, c, :, 2 * n:2 * n + 8].rearrange("p e c -> p c e"),
                               t_ps[u % 2][:].rearrange("p (c e) -> p c e", e=EXPERTS), ACT.Copy).then_inc(t_read, 1)
            act.wait_ge(dest_in, 32)
            with act.Fori(0, N_TURNS // 2) as i:
                for parity in range(2):
                    act.wait_ge(gate_ready, i * 2 + parity + 1)
                    act.wait_ge(h_done, i * 2 + parity)
                    act.activation(th[:], gate_ps[0:FF, 0:TURN * SLOTS], ACT.Tanh, scale=0.5).then_inc(tanh_done, 1)
                    for q in range(2):
                        act.wait_ge(added[q], i * (16 * TURN))
                    for u in range(TURN // 2):
                        act.wait_ge(y_ready, i * TURN + parity * (TURN // 2) + u + 1)
                        for q in range(2):
                            last = act.activation(y[:, parity, 2 * u + q], y_ps[u % 2][0:SLOTS, q * HID:(q + 1) * HID], ACT.Copy,
                                                  scale=w_dest[:, bass.ds(i * (2 * TURN) + parity * TURN + 2 * u + q, 1)])
                        last.then_inc(y_read, 1)

        @block.tensor
        def _(pe):
            pe.wait_ge(consts_in, 4 * 16)
            pe.wait_ge(row_ready, 1)
            pe.transpose(gate_ps[0:BLOCKS, 0:P], row_f[:], ident[:]).then_inc(by_slot_ready, 1)
            for u in range(UNITS_T):
                c, n = u % 2, 4 * (u // 2)
                for g in range((n + 3) // GATHERS + 1):
                    pe.wait_ge(gathered_in[g], 16 * GATHERS)
                if u >= 2:
                    pe.wait_ge(t_read, u - 1)
                for k in range(4):
                    last = pe.transpose(t_ps[u % 2][:, k * P:(k + 1) * P], gathered[:, n + k, c * P:(c + 1) * P], ident[:])
                last.then_inc(t_ready, 1)
            pe.wait_ge(w_ready, 1)
            pe.transpose(up_ps[0:BLOCKS, 0:P], w_slot[:], ident[:]).then_inc(by_slot_ready, 1)
            pe.wait_ge(t_read, UNITS_T)
            pe.wait_ge(by_slot_done, 2)
            with pe.Fori(0, N_TURNS // 2) as i:
                for parity in range(2):
                    pe.wait_ge(wi_in[parity], i * 16 + 16)
                    pe.wait_ge(h_done, i * 2 + parity)
                    for k, (bank, ready) in enumerate(((gate_ps, gate_ready), (up_ps, up_ready))):
                        for e in range(TURN):
                            for c in range(NC):
                                col = (k * NC + c) * FF
                                slots = xsT[:, c, bass.ds(i * (2 * TURN) + parity * TURN + e, 1)].rearrange("p e c -> p (e c)")
                                last = pe.matmul(bank[0:FF, e * SLOTS:(e + 1) * SLOTS], w_in[:, parity, e, col:col + FF], slots,
                                                 start=(c == 0), stop=(c == NC - 1))
                        last.then_inc(ready, 1)
                    pe.wait_ge(wd_in[parity], i * 16 + 16)
                    pe.wait_ge(h_done, i * 2 + parity + 1)
                    for u in range(TURN // 2):
                        pe.wait_ge(y_read, i * TURN + parity * (TURN // 2) + max(u - 1, 0))
                        for q in range(2):
                            e = 2 * u + q
                            last = pe.matmul(y_ps[u % 2][0:SLOTS, q * HID:(q + 1) * HID], h[:, e * SLOTS:(e + 1) * SLOTS],
                                             w_down[:, parity, e], start=True, stop=True)
                        last.then_inc(y_ready, 1)


def finish(nc, x1_rows, sums, out):
    with ExitStack() as ctx:
        def sb(name, shape, dt=F32):
            return ctx.enter_context(nc.sbuf_tensor("f_" + name, shape, dt))

        def sem(name):
            return ctx.enter_context(nc.semaphore("f_" + name))

        x1, m0, m1 = (sb(n, [P, B, NT, HID]) for n in ("x1", "m0", "m1"))
        tmp = (sb("stats", [P, NT, 6]), sb("mv", [P, NT, 2]), sb("var", [P, NT]), sb("guess", [P, NT]), sb("newton", [P, NT]))
        loaded = [sem(f"loaded{b}") for b in range(B)]
        summed, chain, done, stored = sem("summed"), sem("chain"), sem("done"), sem("stored")
        block = ctx.enter_context(nc.Block())
        tiles = lambda a: a.rearrange("(t p) n -> p t n", p=P)

        @block.sync
        def _(sp):
            for b in range(B):
                sp.dma_start(m0[:, b], tiles(sums[0][b * SEQ:(b + 1) * SEQ])).then_inc(loaded[b], 16)
                sp.dma_start(m1[:, b], tiles(sums[1][b * SEQ:(b + 1) * SEQ])).then_inc(loaded[b], 16)
                sp.dma_start(x1[:, b], x1_rows[b]).then_inc(loaded[b], 16)
            for b in range(B):
                sp.wait_ge(done, b + 1)
                sp.dma_start(out[b].rearrange("(t p) n -> p t n", p=P), x1[:, b]).then_inc(stored, 16)
            sp.wait_ge(stored, 16 * B)

        @block.gpsimd
        def _(pool):
            for b in range(B):
                pool.wait_ge(loaded[b], 48)
                pool.tensor_tensor(m0[:, b], m0[:, b], m1[:, b], ALU.add).then_inc(summed, 1)

        @block.vector
        def _(dve):
            link = Links(dve, chain, 0, 0)
            for b in range(B):
                dve.wait_ge(summed, b + 1)
                layer_norm(dve, link, m0[:, b], m0[:, b], tmp, lambda: None)
                dve.tensor_tensor(x1[:, b], x1[:, b], m0[:, b], ALU.add).then_inc(done, 1)


def build(nc, args, out):
    x, wpack = args["x"], args["wpack"]
    w_split = nc.dram_tensor("w_split", (KV_HEADS, P, 2 * WPACK), F32).ap()
    xT_split = nc.dram_tensor("xT_split", (B, P, 2 * NC * SEQ), F32).ap()
    y_parts = nc.dram_tensor("y_parts", (TURNS, P, NT, HID), F32).ap()
    x1_rows = nc.dram_tensor("x1_rows", (B, P, NT, HID), F32).ap()
    rows = nc.dram_tensor("rows", (TOKENS + TRASH, ROW), F32).ap()
    sums = [nc.dram_tensor(f"sums{i}", (TOKENS + TRASH, HID), F32).ap() for i in range(2)]
    slot_info = nc.dram_tensor("slot_info", (P, BLOCKS, 3), F32).ap()
    slot_rows = nc.dram_tensor("slot_rows", (EXPERTS * SLOTS,), I32).ap()
    slot_weights = nc.dram_tensor("slot_weights", (EXPERTS * SLOTS,), F32).ap()
    prepare(nc, x, wpack, args, w_split, xT_split, rows, sums)
    attention(nc, args, w_split, xT_split, y_parts)
    route(nc, x, y_parts, args, x1_rows, rows, sums[0], slot_info)
    experts(nc, args, rows, slot_info, slot_rows, slot_weights, args["expert_w"], sums)
    finish(nc, x1_rows, sums, out)


def lay_out(inputs):
    f = lambda n: np.asarray(inputs[n])
    wq, wk, wv, wo = (f("L0_attn_" + n) for n in ("Wq", "Wk", "Wv", "Wo"))

    def halves(w):
        return w.reshape(-1, HD // 2, 2, HID).transpose(0, 2, 1, 3).reshape(-1, HD, HID)

    q, k, v_ = halves(wq), halves(wk), wv.reshape(KV_HEADS, HD, HID)
    packs = []
    for g in range(KV_HEADS):
        a = np.stack([k[g], v_[g], q[4 * g], q[4 * g + 1]])
        b = q[4 * g + 2:4 * g + 4]
        at = a.reshape(-1, NC, P).transpose(2, 1, 0).reshape(P, -1)
        bt = b.reshape(-1, NC, P).transpose(2, 1, 0).reshape(P, -1)
        o = wo[:, 512 * g:512 * g + 512].reshape(HID, GROUP, HD).transpose(2, 1, 0).reshape(P, -1)
        packs.append(np.concatenate([at, bt, o], 1))
    arrays = {"x": f("L0_attn_x"), "wpack": np.stack(packs)}
    freq = np.float32(1) / np.power(10000.0, np.arange(0, HD, 2) / HD).astype(np.float32)
    angle = (np.arange(SEQ, dtype=np.float32)[:, None] * freq[None]).astype(np.float64)
    s = float(HD) ** -0.25
    cos = np.concatenate([np.cos(angle), np.cos(angle)], 1) * s
    sin = np.concatenate([np.sin(angle), -np.sin(angle)], 1) * s
    lay = lambda a: np.ascontiguousarray(a.reshape(NT, P, HD).transpose(1, 0, 2)).astype(np.float32)
    arrays["cos"], arrays["sin"] = lay(cos), lay(sin)
    arrays["ident"] = np.eye(P, dtype=np.float32)
    arrays["ident_bf"] = np.eye(P).astype(mybir.dt.np(BF16))
    arrays["mask_bf"] = np.triu(np.full((P, P), NEG), 1).astype(mybir.dt.np(BF16))
    g = lambda n: np.asarray(inputs["L0_ffn_" + n])
    chunks = lambda w: w.reshape(NC, P, -1).transpose(1, 0, 2)
    arrays["gate_w"] = chunks(g("gate_w"))
    arrays["bias"] = np.broadcast_to(g("bias"), (P, EXPERTS))
    arrays["ws_in"] = np.stack([chunks(g("ws_gate")), chunks(g("ws_up"))], 1)
    arrays["ws_down"] = g("ws_down")
    w_in = np.stack([g("w_gate"), g("w_up")], 1).reshape(EXPERTS, 2, NC, P, FF).transpose(0, 3, 1, 2, 4).reshape(EXPERTS, P, -1)
    w_down = np.concatenate([g("w_down"), np.zeros((EXPERTS, P - FF, HID), np.float32)], 1)
    arrays["expert_w"] = np.concatenate([w_in, w_down], 2)
    bf = mybir.dt.np(BF16)
    lower = np.arange(GROUPS_R)[None] < np.arange(GROUPS_R)[:, None]
    arrays["lower"] = np.broadcast_to(lower.reshape(-1), (P, GROUPS_R ** 2)).astype(np.float32)
    arrays["tri"] = np.triu(np.ones((P, P)), 1).astype(bf)
    arrays["ones"] = np.ones((P, P)).astype(bf)
    p, t = np.meshgrid(np.arange(P), np.arange(B * NT), indexing="ij")
    arrays["token"] = np.stack([p, t, np.ones_like(p), np.zeros_like(p)], 2).reshape(P, -1).astype(bf)
    arrays["slot_c"] = np.broadcast_to(np.arange(SLOTS)[None, :, None], (P, SLOTS, EXPERTS)).astype(bf)
    arrays["diag"] = (np.arange(P)[:, None] % EXPERTS == np.arange(EXPERTS)[None]).astype(np.float32)
    arrays["trash"] = (TOKENS + 2 * np.arange(BLOCKS)[None] + np.arange(P)[:, None] // EXPERTS).astype(np.float32)
    return {n: np.ascontiguousarray(a) for n, a in arrays.items()}


def kernel(**inputs):
    import concourse.bacc as _bacc
    from concourse.bass_utils import run_bass_kernel_spmd as _run

    nc = _bacc.Bacc("TRN2", target_bir_lowering=False, num_devices=1)
    arrays = lay_out(inputs)
    args = {n: nc.dram_tensor(f"in_{n}", a.shape, mybir.dt.from_np(a.dtype), kind="ExternalInput").ap()
            for n, a in arrays.items()}
    out = nc.dram_tensor("out", (B, SEQ, HID), F32, kind="ExternalOutput").ap()
    build(nc, args, out)
    r = _run(nc, [{f"in_{n}": a for n, a in arrays.items()}], core_ids=[0])
    return np.asarray(r.results[0]["out"])
```

```python
from contextlib import ExitStack

import numpy as np

import concourse.bass as bass
from concourse import mybir

F32 = mybir.dt.float32
F32R = mybir.dt.float32r
BF16 = mybir.dt.bfloat16
I32 = mybir.dt.int32
ALU = mybir.AluOpType
ACT = mybir.ActivationFunctionType
AX = mybir.AxisListType

P = 128
B, SEQ, HID = 4, 1024, 256
HEADS, KV_HEADS, HD = 16, 4, 128
GROUP = HEADS // KV_HEADS
NT = SEQ // P
NC = HID // P
EPS = 1e-5
NEG = -1e30

WA = NC * 4 * HD
WB = NC * 2 * HD
WO = GROUP * HID
WPACK = WA + WB + WO

STEPS = GROUP * NT
BODY = KV_HEADS * STEPS
PAIRS = BODY // 2
ROT = 32
NORM_AT = BODY + 4
RESIDUAL_AT, NORM2_AT = NORM_AT + 9, NORM_AT + 12
ROWS_AT = NORM2_AT + 9
NORM_END = ROWS_AT + 3
UNITS_BEFORE = [0, 1, 2, 3, 4, 6, 8, 10]
UNITS = 12


def prepare(nc, x, wpack, consts, w_split, xT_split, rows, sums):
    with ExitStack() as ctx:
        def sb(name, shape, dt=F32):
            return ctx.enter_context(nc.sbuf_tensor(name, shape, dt))

        def sem(name):
            return ctx.enter_context(nc.semaphore(name))

        ident = sb("pre_ident", [P, P])
        w_raw = sb("w_raw", [P, 2, WPACK])
        w_hl = sb("w_hl", [P, 2, 2, WPACK], F32R)
        x_raw = sb("x_raw", [P, 2, NT, HID])
        x_n = sb("x_n", [P, 2, NT, HID])
        stats = sb("pre_stats", [P, B, NT, 6])
        mv = sb("pre_mv", [P, B, NT, 2])
        var, std, rstd = (sb("pre_" + n, [P, B, NT]) for n in ("var", "std", "rstd"))
        xT = sb("pre_xT", [P, 2, 2, NC, SEQ], F32R)
        banks = [ctx.enter_context(nc.psum_tensor(f"pre_ps{i}", [P, 512], F32)) for i in range(2)]

        ident_in = sem("pre_ident_in")
        x_in = [sem(f"x_in{i}") for i in range(2)]
        w_in = [sem(f"w_in{i}") for i in range(2)]
        w_out = [sem(f"w_out{i}") for i in range(2)]
        xT_out = [sem(f"xT_out{i}") for i in range(2)]
        w_hi, w_lo = sem("w_hi"), sem("w_lo")
        stats_done, mv_done, xn_done = sem("pre_stats_done"), sem("pre_mv_done"), sem("xn_done")
        var_done, std_done, rstd_done = sem("pre_var_done"), sem("pre_std_done"), sem("pre_rstd_done")
        t_ready, t_hi, t_lo = sem("pre_t_ready"), sem("pre_t_hi"), sem("pre_t_lo")

        zeros = sb("pre_zeros", [P, NT * HID])
        zeroed, zeros_out = sem("pre_zeroed"), sem("zeros_out")

        block = ctx.enter_context(nc.Block())

        @block.gpsimd
        def _(pool):
            pool.memset(zeros[:], 0.0).then_inc(zeroed, 1)
            pool.wait_ge(zeroed, 1)
            pool.dma_start(rows[TOKENS:], zeros[0:TRASH, 0:HID + EXPERTS]).then_inc(zeros_out, 16)
            pool.dma_start(sums[0][TOKENS:], zeros[0:TRASH, 0:HID]).then_inc(zeros_out, 16)
            pool.dma_start(sums[1][TOKENS:], zeros[0:TRASH, 0:HID]).then_inc(zeros_out, 16)
            for b in range(B):
                pool.dma_start(sums[1][b * SEQ:(b + 1) * SEQ].rearrange("(p t) n -> p (t n)", p=P), zeros[:]).then_inc(zeros_out, 16)
            pool.wait_ge(zeros_out, 16 * (B + 3))

        units = [(c, half) for half in range(2) for c in range(NC)]

        @block.sync
        def _(sp):
            sp.dma_start(ident[:], consts["ident"]).then_inc(ident_in, 16)
            for b in range(B):
                if b >= 2:
                    sp.wait_ge(xn_done, NT * (b - 1))
                sp.dma_start(x_raw[:, b % 2], x[b].rearrange("(t p) n -> p t n", p=P)).then_inc(x_in[b % 2], 16)
                if b >= 2:
                    sp.wait_ge(w_lo, b - 1)
                sp.dma_start(w_raw[:, b % 2], wpack[b]).then_inc(w_in[b % 2], 16)
            for b in range(B):
                sp.wait_ge(t_lo, len(units) * (b + 1))
                sp.dma_start(xT_split[b], xT[:, b % 2].rearrange("p s c n -> p (s c n)").bitcast(F32)).then_inc(xT_out[b % 2], 16)
                sp.wait_ge(w_lo, b + 1)
                sp.dma_start(w_split[b], w_hl[:, b % 2].rearrange("p s n -> p (s n)").bitcast(F32)).then_inc(w_out[b % 2], 16)
            for i in range(2):
                sp.wait_ge(xT_out[i], 32)
                sp.wait_ge(w_out[i], 32)

        @block.vector
        def _(dve):
            for b in range(B):
                dve.wait_ge(x_in[b % 2], 16 * (b // 2 + 1))
                for t in range(NT):
                    dve.bn_stats(stats[:, b, t], x_raw[:, b % 2, t]).then_inc(stats_done, 1)
                dve.wait_ge(stats_done, NT * (b + 1))
                for t in range(NT):
                    dve.bn_aggr(mv[:, b, t], stats[:, b, t]).then_inc(mv_done, 1)
                dve.wait_ge(mv_done, NT * (b + 1))
                dve.tensor_scalar(var[:, b], mv[:, b, :, 1], EPS, None, ALU.add).then_inc(var_done, 1)
                dve.wait_ge(std_done, b + 1)
                dve.reciprocal(rstd[:, b], std[:, b]).then_inc(rstd_done, 1)
                dve.wait_ge(rstd_done, b + 1)
                if b >= 2:
                    dve.wait_ge(t_ready, len(units) * (b - 1))
                for t in range(NT):
                    dve.tensor_scalar(x_n[:, b % 2, t], x_raw[:, b % 2, t], mv[:, b, t, 0:1], rstd[:, b, t:t + 1],
                                      ALU.subtract, ALU.mult).then_inc(xn_done, 1)
                dve.wait_ge(w_hi, b + 1)
                if b >= 2:
                    dve.wait_ge(w_out[b % 2], 16)
                dve.tensor_tensor(w_hl[:, b % 2, 1], w_raw[:, b % 2], w_hl[:, b % 2, 0].bitcast(F32),
                                  ALU.subtract).then_inc(w_lo, 1)
                for u, (c, half) in enumerate(units):
                    dve.wait_ge(t_hi, len(units) * b + u + 1)
                    cols = slice(512 * half, 512 * half + 512)
                    dve.tensor_tensor(xT[:, b % 2, 1, c, cols], banks[u % 2][:],
                                      xT[:, b % 2, 0, c, cols].bitcast(F32), ALU.subtract).then_inc(t_lo, 1)

        @block.scalar
        def _(act):
            for b in range(B):
                act.wait_ge(var_done, b + 1)
                act.activation(std[:, b], var[:, b], ACT.Sqrt).then_inc(std_done, 1)
                act.wait_ge(w_in[b % 2], 16 * (b // 2 + 1))
                if b >= 2:
                    act.wait_ge(w_out[b % 2], 16)
                act.activation(w_hl[:, b % 2, 0], w_raw[:, b % 2], ACT.Copy).then_inc(w_hi, 1)
                for u, (c, half) in enumerate(units):
                    act.wait_ge(t_ready, len(units) * b + u + 1)
                    if b >= 2 and u == 0:
                        act.wait_ge(xT_out[b % 2], 16)
                    act.activation(xT[:, b % 2, 0, c, 512 * half:512 * half + 512], banks[u % 2][:],
                                   ACT.Copy).then_inc(t_hi, 1)

        @block.tensor
        def _(pe):
            pe.wait_ge(ident_in, 16)
            for b in range(B):
                for u, (c, half) in enumerate(units):
                    n = len(units) * b + u
                    pe.wait_ge(xn_done, NT * b + 4 * half + 4)
                    if n >= 2:
                        pe.wait_ge(t_lo, n - 1)
                    for i in range(4):
                        last = pe.transpose(banks[u % 2][:, i * P:(i + 1) * P],
                                            x_n[:, b % 2, 4 * half + i, c * P:(c + 1) * P], ident[:])
                    last.then_inc(t_ready, 1)


def attention(nc, consts, x, w_split, xT_split, x1_rows, rows):
    with ExitStack() as ctx:
        def sb(name, shape, dt=F32):
            return ctx.enter_context(nc.sbuf_tensor(name, shape, dt))

        def sem(name):
            return ctx.enter_context(nc.semaphore(name))

        ident = sb("ident", [P, P])
        ident_bf = sb("ident_bf", [P, P], BF16)
        mask_bf = sb("mask_bf", [P, P], BF16)
        cos_t = sb("cos_t", [P, NT, HD])
        sin_t = sb("sin_t", [P, NT, HD])
        xT = sb("xT", [P, 2, NC, SEQ], F32R)
        w_a = sb("w_a", [P, 2, NC, 4 * HD], F32R)
        w_b = sb("w_b", [P, 2, NC, 2 * HD], F32R)
        w_o = sb("w_o", [P, 2, 2, GROUP, HID], F32R)
        qT = sb("qT", [P, 2, 2, 2, SEQ], F32R)
        kT = sb("kT", [P, 2, 2, SEQ], F32R)
        v = sb("v", [P, 2, 2, NT, HD], F32R)
        probs = sb("probs", [P, 4, SEQ])
        pT = sb("pT", [P, 2, 2, NT, 2 * P], F32R)
        avT = sb("avT", [P, 2, 2 * P], F32R)
        y = sb("y", [P, NT, HID])
        y_whole = sb("y_whole", [P, NT, HID])
        xb = sb("xb", [P, NT, HID])
        norm_tmp = (sb("stats", [P, NT, 6]), sb("mv", [P, NT, 2]), sb("var", [P, NT]), sb("guess", [P, NT]),
                    sb("newton", [P, NT]))
        y_part = sb("y_part", [P, 2, 2, HID])
        rope_c = sb("rope_c", [P, 512])
        rope_s = sb("rope_s", [P, 512])
        roped = sb("roped", [P, 512])
        neg_max = sb("neg_max", [P, 16])
        row_sum = sb("row_sum", [P, 16])
        inv_sum = sb("inv_sum", [P, 16])

        s_ps = ctx.enter_context(nc.psum_tensor("s_ps", [P, 2, SEQ], F32))
        t_ps = [ctx.enter_context(nc.psum_tensor(f"t_ps{i}", [P, 512], F32)) for i in range(2)]
        av_ps = ctx.enter_context(nc.psum_tensor("av_ps", [P, 512], F32))
        prod_ps = ctx.enter_context(nc.psum_tensor("prod_ps", [P, 512], F32))

        consts_in, bf_done = sem("consts_in"), sem("bf_done")
        xT_in, xT_landed, wa_in, wb_in = sem("xT_in"), sem("xT_landed"), sem("wa_in"), sem("wb_in")
        wo_in = [sem(f"wo_in{i}") for i in range(2)]
        wa_used, wb_used, wo_used = sem("wa_used"), sem("wb_used"), sem("wo_used")
        qkv_ready = sem("qkv_ready")
        bank_read = sem("bank_read")
        rope_added = sem("rope_added")
        qk_ready = sem("qk_ready")
        qk_hi, qk_lo = sem("qk_hi"), sem("qk_lo")
        v_hi = sem("v_hi")
        scores_ready, max_ready, exp_done = sem("scores_ready"), sem("max_ready"), sem("exp_done")
        pT_ready, pT_hi, pT_lo = sem("pT_ready"), sem("pT_hi"), sem("pT_lo")
        av_ready, av_hi, av_lo = sem("av_ready"), sem("av_hi"), sem("av_lo")
        inv_ready, op_ready, part_done, y_done = sem("inv_ready"), sem("op_ready"), sem("part_done"), sem("y_done")
        y_free = sem("y_free")
        norm_chain, stats_settled, y_normed = sem("norm_chain"), sem("stats_settled"), sem("y_normed")
        x_in, x1_done, x1_out, x2_done, x2_out = (sem(n) for n in ("xb_in", "x1_done", "x1_out", "x2_done", "x2_out"))

        block = ctx.enter_context(nc.Block())

        def wait(eng, semaphore, turn, per_turn, at_least):
            if isinstance(turn, int):
                if per_turn * turn + at_least > 0:
                    eng.wait_ge(semaphore, per_turn * turn + at_least)
            else:
                assert at_least >= 0, (semaphore, at_least)
                eng.wait_ge(semaphore, turn * per_turn + max(at_least, 1))

        def tile(k):
            return k % NT

        def units_before(k):
            return (k // NT) * UNITS + UNITS_BEFORE[k % NT]

        def step_units(k):
            blocks = tile(k) + 1
            return [(units_before(k) + u, 4 * u, min(4, blocks - 4 * u)) for u in range((blocks + 3) // 4)]

        AT = {0: ("this", 8), 3: ("this", 9), 6: ("this", 10), 8: ("this", 11),
              11: ("next", 0), 14: ("next", 1), 16: ("next", 2), 19: ("next", 3),
              22: ("next", 4), 24: ("next", 5), 27: ("next", 6), 30: ("next", 7)}

        def produced_at(k):
            if k < 0 or k % STEPS not in AT:
                return None
            when, unit = AT[k % STEPS]
            return k // STEPS + (when == "next"), unit

        def program(eng, slot):
            for k in range(-1, ROT):
                slot(k, 0, False)
            with eng.Fori(0, B - 1) as turn:
                for k in range(ROT, ROT + BODY):
                    slot(k, turn, False)
            for k in range(ROT, NORM_END):
                slot(k, B - 1, True)

        def exists(k, turn, last):
            return k >= 0 and not (last and k >= BODY)

        def made(group, last):
            return not (last and group >= KV_HEADS)

        def destination(group, unit):
            cols = slice(256 * (unit % 4), 256 * (unit % 4) + 256)
            if unit < 4:
                return kT[:, group % 2, 0, cols], kT[:, group % 2, 1, cols], prod_ps[:, 0:256]
            pair = (unit - 4) // 4
            return (qT[:, pair, 0, :, cols], qT[:, pair, 1, :, cols],
                    prod_ps[:].rearrange("p (h n) -> p h n", h=2))

        @block.sync
        def _(sp):
            for dst, name in ((ident, "ident"), (cos_t, "cos"), (sin_t, "sin")):
                sp.dma_start(dst[:], consts[name]).then_inc(consts_in, 16)
            sp.dma_start(ident_bf[:], consts["ident_bf"]).then_inc(consts_in, 16)
            sp.dma_start(mask_bf[:], consts["mask_bf"]).then_inc(consts_in, 16)
            def load(b):
                later = not isinstance(b, int)
                if later:
                    sp.wait_ge(qkv_ready, b * (KV_HEADS * UNITS))
                sp.dma_start(xT[:].rearrange("p s c n -> p (s c n)").bitcast(F32), xT_split[b]).then_inc(xT_in, 16)
                sp.wait_ge(xT_in, b * 16 + 16)
                sp.sem_inc(xT_landed, 1)
                for g in range(KV_HEADS):
                    src = w_split[g].rearrange("p (s n) -> p s n", s=2)
                    if later or g:
                        sp.wait_ge(wa_used, b * KV_HEADS + g)
                    sp.dma_start(w_a[:].rearrange("p s c n -> p s (c n)").bitcast(F32), src[:, :, 0:WA]).then_inc(wa_in, 16)
                    if later or g:
                        sp.wait_ge(wb_used, b * KV_HEADS + g)
                    sp.dma_start(w_b[:].rearrange("p s c n -> p s (c n)").bitcast(F32), src[:, :, WA:WA + WB]).then_inc(wb_in, 16)
                    if later or g >= 2:
                        sp.wait_ge(wo_used, b * KV_HEADS + g - 1)
                    sp.dma_start(w_o[:, g % 2].rearrange("p s h n -> p s (h n)").bitcast(F32),
                                 src[:, :, WA + WB:WPACK]).then_inc(wo_in[g % 2], 16)

            load(0)
            with sp.Fori(0, B - 1) as b:
                load(b + 1)

        @block.tensor
        def _(pe):
            pe.wait_ge(consts_in, 5 * 16)

            def project(group, unit, turn):
                wait(pe, qk_lo, turn, KV_HEADS * UNITS, UNITS * group + unit)
                if unit in (0, 4):
                    wait(pe, wa_in, turn, 16 * KV_HEADS, 16 * (group + 1))
                if unit == 8:
                    wait(pe, wb_in, turn, 16 * KV_HEADS, 16 * (group + 1))
                w = w_b if unit >= 8 else w_a
                cols = slice(2 * HD, 4 * HD) if 4 <= unit < 8 else slice(0, 2 * HD)
                for i in range(2):
                    rows = slice((2 * (unit % 4) + i) * P, (2 * (unit % 4) + i + 1) * P)
                    passes = [(c, a, s) for c in range(NC) for a, s in ((0, 0), (0, 1), (1, 0))]
                    for n, (c, a, s) in enumerate(passes):
                        last = pe.matmul(prod_ps[:, i * 256:(i + 1) * 256], xT[:, a, c, rows], w[:, s, c, cols],
                                         start=(n == 0), stop=(n == len(passes) - 1))
                last.then_inc(qkv_ready, 1)

            def project_done(unit):
                if unit == 7:
                    pe.sem_inc(wa_used, 1)
                if unit == 11:
                    pe.sem_inc(wb_used, 1)

            def transpose_unit(group, unit, turn):
                wait(pe, rope_added, turn, KV_HEADS * UNITS, UNITS * group + unit + 1)
                heads = 1 if unit < 4 else 2
                for h in range(heads):
                    for i in range(2):
                        src = roped[:, i * heads * HD + h * HD:i * heads * HD + (h + 1) * HD]
                        last = pe.transpose(prod_ps[:, h * 256 + i * P:h * 256 + (i + 1) * P], src, ident[:])
                last.then_inc(qk_ready, 1)

            def scores(k, turn):
                group, h, i = k // STEPS, (k % STEPS) // NT, tile(k)
                wait(pe, exp_done, turn, BODY, k - 1)
                if h % 2 == 0 and i % 2 == 0:
                    wait(pe, qk_lo, turn, KV_HEADS * UNITS, UNITS * group + 4 + 4 * (h // 2) + i // 2 + 1)
                rows = slice(i * P, (i + 1) * P)
                width = (i + 1) * P
                for lo in range(0, width, 512):
                    hi = min(width, lo + 512)
                    out = s_ps[:, k % 2, lo:hi]
                    for n, (a, s) in enumerate(((0, 0), (0, 1), (1, 0))):
                        if n == 2 and hi == width:
                            pe.matmul(s_ps[:, k % 2, width - P:width], ident_bf[:], mask_bf[:], start=False, stop=False)
                        last = pe.matmul(out, qT[:, h // 2, a, h % 2, rows], kT[:, group % 2, s, lo:hi],
                                         start=(n == 0), stop=(n == 2))
                last.then_inc(scores_ready, 1)

            def transpose_probs(k, turn):
                wait(pe, exp_done, turn, BODY, k + 1)
                for n, first, count in step_units(k):
                    wait(pe, pT_lo, turn, BODY // NT * UNITS, n - 1)
                    for j in range(count):
                        last = pe.transpose(t_ps[n % 2][:, j * P:(j + 1) * P],
                                            probs[:, k % 4, (first + j) * P:(first + j + 1) * P], ident[:])
                    last.then_inc(pT_ready, 1)

            def attend(n, turn):
                group, p = n // 16, n % 4
                wait(pe, pT_lo, turn, BODY // NT * UNITS, units_before(2 * n + 2))
                wait(pe, part_done, turn, PAIRS, n)
                for j in range(2 * p + 2):
                    cols = slice(P if j == 2 * p + 1 else 0, 2 * P)
                    for m, (a, s) in enumerate(((0, 0), (0, 1), (1, 0))):
                        last = pe.matmul(av_ps[:, cols], v[:, group % 2, a, j], pT[:, n % 2, s, j, cols],
                                         start=(j == 0 and m == 0), stop=(j == 2 * p + 1 and m == 2),
                                         skip_group_check=True)
                last.then_inc(av_ready, 1)

            def output(n, turn):
                group, h = n // 16, (n % 16) // 4
                wait(pe, av_lo, turn, PAIRS, n + 1)
                if n % 16 == 0:
                    wait(pe, wo_in[group % 2], turn, 8 * KV_HEADS, 16 * (group // 2 + 1))
                for i in range(2):
                    for m, (a, s) in enumerate(((0, 0), (0, 1), (1, 0))):
                        last = pe.matmul(av_ps[:, i * HID:(i + 1) * HID], avT[:, a, i * P:(i + 1) * P],
                                         w_o[:, group % 2, s, h], start=(m == 0), stop=(m == 2))
                last.then_inc(op_ready, 1)
                if n % 16 == 15:
                    pe.wait_ge(op_ready, turn * PAIRS + n + 1)
                    pe.sem_inc(wo_used, 1)

            def slot(k, turn, last):
                if exists(k + 1, turn, last):
                    scores(k + 1, turn)
                now, before = produced_at(k), produced_at(k - 2)
                if before and made(before[0], last):
                    transpose_unit(*before, turn)
                if exists(k - 1, turn, last):
                    transpose_probs(k - 1, turn)
                if k % 2 and k >= 3 and exists(k - 3, turn, last):
                    attend((k - 3) // 2, turn)
                if k % 2 == 0 and k >= 4 and exists(k - 4, turn, last):
                    output((k - 4) // 2, turn)
                if now and made(now[0], last):
                    project(*now, turn)
                    if now[1] in (7, 11):
                        wait(pe, qkv_ready, turn, KV_HEADS * UNITS, UNITS * now[0] + now[1] + 1)
                        project_done(now[1])

            for unit in range(8):
                project(0, unit, 0)
                if unit == 7:
                    pe.wait_ge(qkv_ready, 8)
                    project_done(7)
                transpose_unit(0, unit, 0)
            program(pe, slot)

        @block.vector
        def _(dve):
            dve.wait_ge(consts_in, 5 * 16)

            def settled():
                dve.sem_inc(stats_settled, 1)

            def rope(group, unit, turn):
                n = UNITS * group + unit
                j = unit % 4
                wait(dve, qkv_ready, turn, KV_HEADS * UNITS, n + 1)
                wait(dve, rope_added, turn, KV_HEADS * UNITS, n)
                if unit < 4:
                    src = prod_ps[:].rearrange("p (t n) -> p t n", t=2)
                    for out, table in ((rope_c, cos_t), (rope_s, sin_t)):
                        dve.tensor_tensor(out[:, 0:256].rearrange("p (t n) -> p t n", t=2), src[:, :, 0:HD],
                                          table[:, 2 * j:2 * j + 2], ALU.mult)
                    wait(dve, av_ready, turn, PAIRS, 16 * (group - 1))
                    hi, lo = (v[:, group % 2, s, 2 * j:2 * j + 2] for s in range(2))
                    dve.tensor_copy(hi, src[:, :, HD:2 * HD]).then_inc(v_hi, 1)
                    wait(dve, v_hi, turn, 4 * KV_HEADS, 4 * group + j + 1)
                    dve.tensor_tensor(lo, src[:, :, HD:2 * HD], hi.bitcast(F32), ALU.subtract).then_inc(bank_read, 1)
                else:
                    src = prod_ps[:].rearrange("p (t h n) -> p t h n", t=2, h=2)
                    for out, table in ((rope_c, cos_t), (rope_s, sin_t)):
                        tab = table[:, 2 * j:2 * j + 2].unsqueeze(2).broadcast_to([P, 2, 2, HD])
                        last = dve.tensor_tensor(out[:].rearrange("p (t h n) -> p t h n", t=2, h=2), src, tab, ALU.mult)
                    last.then_inc(bank_read, 1)

            def qk_low(group, unit, turn):
                wait(dve, qk_hi, turn, KV_HEADS * UNITS, UNITS * group + unit + 1)
                hi, lo, src = destination(group, unit)
                dve.tensor_tensor(lo, src, hi.bitcast(F32), ALU.subtract).then_inc(qk_lo, 1)

            def row_max(k, turn):
                wait(dve, scores_ready, turn, BODY, k + 1)
                dve.reduce_max(neg_max[:, k % 16:k % 16 + 1], s_ps[:, k % 2, 0:(tile(k) + 1) * P], AX.X,
                               negate=True).then_inc(max_ready, 1)

            def probs_low(k, turn):
                for n, first, count in step_units(k):
                    wait(dve, pT_hi, turn, BODY // NT * UNITS, n + 1)
                    hi, lo = (pT[:, (k // 2) % 2, s, first:first + count, (k % 2) * P:(k % 2 + 1) * P] for s in range(2))
                    dve.tensor_tensor(lo, t_ps[n % 2][:, 0:count * P].rearrange("p (j n) -> p j n", n=P),
                                      hi.bitcast(F32), ALU.subtract).then_inc(pT_lo, 1)

            def attended_low(n, turn):
                at = (2 * n) % 16
                wait(dve, exp_done, turn, BODY, 2 * n + 2)
                dve.reciprocal(inv_sum[:, at:at + 2], row_sum[:, at:at + 2]).then_inc(inv_ready, 1)
                wait(dve, av_hi, turn, PAIRS, n + 1)
                dve.tensor_tensor(avT[:, 1], av_ps[:, 0:2 * P], avT[:, 0].bitcast(F32), ALU.subtract).then_inc(av_lo, 1)

            def slot(k, turn, last):
                if exists(k + 1, turn, last):
                    row_max(k + 1, turn)
                now, before = produced_at(k), produced_at(k - 2)
                if before and made(before[0], last):
                    qk_low(*before, turn)
                if exists(k - 1, turn, last):
                    probs_low(k - 1, turn)
                if k % 2 and k >= 3 and exists(k - 3, turn, last):
                    attended_low((k - 3) // 2, turn)
                if now and made(now[0], last):
                    rope(*now, turn)
                if NORM_AT <= k < NORM_AT + NORM_STAGES:
                    if k == NORM_AT:
                        dve.wait_ge(y_done, turn * PAIRS + PAIRS)
                    norm_stage(dve, norm_chain, turn, 0, k - NORM_AT, y_whole, y_whole, norm_tmp, settled)
                    if k == NORM_AT + NORM_STAGES - 1:
                        dve.sem_inc(y_normed, 1)
                if NORM2_AT <= k < NORM2_AT + NORM_STAGES:
                    if k == NORM2_AT:
                        dve.wait_ge(x1_done, turn + 1)
                    norm_stage(dve, norm_chain, turn, NORM_LINKS, k - NORM2_AT, y_whole, xb, norm_tmp, settled)
                    if k == NORM2_AT + NORM_STAGES - 1:
                        dve.sem_inc(x2_done, 1)

            for unit in range(8):
                rope(0, unit, 0)
                qk_low(0, unit, 0)
            program(dve, slot)

        @block.scalar
        def _(act):
            def qk_high(group, unit, turn):
                wait(act, qk_ready, turn, KV_HEADS * UNITS, UNITS * group + unit + 1)
                if unit < 4:
                    wait(act, scores_ready, turn, BODY, STEPS * (group - 1))
                elif unit < 8:
                    wait(act, scores_ready, turn, BODY, STEPS * (group - 1) + 2 * NT)
                else:
                    wait(act, scores_ready, turn, BODY, STEPS * group)
                hi, _, src = destination(group, unit)
                act.activation(hi, src, ACT.Copy).then_inc(qk_hi, 1)

            def exponentials(k, turn):
                width = (tile(k) + 1) * P
                wait(act, max_ready, turn, BODY, k + 1)
                wait(act, pT_ready, turn, BODY // NT * UNITS, units_before(k - 3))
                wait(act, inv_ready, turn, PAIRS, k // 2 - 7)
                act.activation(probs[:, k % 4, 0:width], s_ps[:, k % 2, 0:width], ACT.Exp,
                               bias=neg_max[:, k % 16:k % 16 + 1],
                               accum_out=row_sum[:, k % 16:k % 16 + 1]).then_inc(exp_done, 1)

            def probs_high(k, turn):
                for n, first, count in step_units(k):
                    wait(act, pT_ready, turn, BODY // NT * UNITS, n + 1)
                    wait(act, av_ready, turn, PAIRS, k // 2 - 1)
                    act.activation(pT[:, (k // 2) % 2, 0, first:first + count, (k % 2) * P:(k % 2 + 1) * P],
                                   t_ps[n % 2][:, 0:count * P].rearrange("p (j n) -> p j n", n=P),
                                   ACT.Copy).then_inc(pT_hi, 1)

            def attended_high(n, turn):
                wait(act, av_ready, turn, PAIRS, n + 1)
                wait(act, op_ready, turn, PAIRS, n)
                act.activation(avT[:, 0], av_ps[:, 0:2 * P], ACT.Copy).then_inc(av_hi, 1)

            def output_scaled(n, turn):
                wait(act, op_ready, turn, PAIRS, n + 1)
                wait(act, inv_ready, turn, PAIRS, n + 1)
                wait(act, y_done, turn, PAIRS, n - 1)
                for i in range(2):
                    at = (2 * n + i) % 16
                    last = act.activation(y_part[:, n % 2, i], av_ps[:, i * HID:(i + 1) * HID], ACT.Copy,
                                          scale=inv_sum[:, at:at + 1])
                last.then_inc(part_done, 1)

            def slot(k, turn, last):
                before = produced_at(k - 2)
                if before and made(before[0], last):
                    qk_high(*before, turn)
                if exists(k - 1, turn, last):
                    probs_high(k - 1, turn)
                if exists(k + 1, turn, last):
                    exponentials(k + 1, turn)
                if k % 2 and k >= 3 and exists(k - 3, turn, last):
                    attended_high((k - 3) // 2, turn)
                if k % 2 == 0 and k >= 4 and exists(k - 4, turn, last):
                    output_scaled((k - 4) // 2, turn)

            for unit in range(8):
                qk_high(0, unit, 0)
            program(act, slot)

        @block.gpsimd
        def _(pool):
            def rope_add(group, unit, turn):
                n = UNITS * group + unit
                wait(pool, bank_read, turn, KV_HEADS * UNITS, n + 1)
                wait(pool, qk_ready, turn, KV_HEADS * UNITS, n)
                width = 256 if unit < 4 else 512
                out, c, s = (a[:, 0:width].rearrange("p (m n) -> p m n", n=HD) for a in (roped, rope_c, rope_s))
                half = HD // 2
                pool.tensor_tensor(out[:, :, 0:half], c[:, :, 0:half], s[:, :, half:HD], ALU.add)
                pool.tensor_tensor(out[:, :, half:HD], c[:, :, half:HD], s[:, :, 0:half], ALU.add).then_inc(rope_added, 1)

            def add_output(n, turn):
                pair = slice(2 * (n % 4), 2 * (n % 4) + 2)
                wait(pool, part_done, turn, PAIRS, n + 1)
                if n % PAIRS < 4:
                    pool.sem_inc(y_free, 1)
                    pool.tensor_copy(y[:, pair], y_part[:, n % 2]).then_inc(y_done, 1)
                else:
                    wait(pool, y_done, turn, PAIRS, n - 3)
                    out = y_whole if n % PAIRS >= PAIRS - 4 else y
                    pool.tensor_tensor(out[:, pair], y[:, pair], y_part[:, n % 2], ALU.add).then_inc(y_done, 1)

            def norm_part(k, turn, last):
                if k == RESIDUAL_AT:
                    pool.wait_ge(y_normed, turn + 1)
                    pool.wait_ge(x_in, turn * 16 + 16)
                    pool.tensor_tensor(xb[:], xb[:], y_whole[:], ALU.add).then_inc(x1_done, 1)
                if k == RESIDUAL_AT + 1:
                    pool.wait_ge(x1_done, turn + 1)
                    pool.dma_start(x1_rows[turn], xb[:]).then_inc(x1_out, 16)
                if k == ROWS_AT:
                    pool.wait_ge(x2_done, turn + 1)
                    out = rows[bass.ds(turn * SEQ, SEQ), 0:HID] if not last else rows[turn * SEQ:(turn + 1) * SEQ, 0:HID]
                    pool.dma_start(out.rearrange("(t p) n -> p t n", p=P), y_whole[:]).then_inc(x2_out, 16)
                    if not last:
                        pool.wait_ge(x1_out, turn * 16 + 16)
                        pool.dma_start(xb[:], x[turn + 1].rearrange("(t p) n -> p t n", p=P)).then_inc(x_in, 16)
                if k == NORM_END - 1:
                    pool.wait_ge(x2_out, turn * 16 + 16)
                    pool.sem_inc(y_free, 1)

            def slot(k, turn, last):
                now = produced_at(k)
                if now and made(now[0], last):
                    rope_add(*now, turn)
                if k % 2 == 0 and k >= 4 and exists(k - 4, turn, last):
                    add_output((k - 4) // 2, turn)
                norm_part(k, turn, last)

            pool.dma_start(xb[:], x[0].rearrange("(t p) n -> p t n", p=P)).then_inc(x_in, 16)
            for unit in range(8):
                rope_add(0, unit, 0)
            program(pool, slot)
            pool.wait_ge(x1_out, 16 * B)
            pool.wait_ge(x2_out, 16 * B)


TRASH = 48
EXPERTS, TOP, FF = 64, 6, 96
GROUPS_R, TOP_GROUPS = 8, 4
SLOTS = 48
SCALE = 2.5
TOKENS = B * SEQ
BLOCKS = EXPERTS * SLOTS // P
ROW = HID + EXPERTS
RSQRT_STEPS = 4
SELECT_LINKS, PLACE_LINKS = 25, 4


class Links:

    def __init__(self, eng, semaphore, turn, per_turn):
        self.eng, self.semaphore, self.turn, self.per_turn, self.n = eng, semaphore, turn, per_turn, 0

    def __call__(self, instruction):
        instruction.then_inc(self.semaphore, 1)
        self.n += 1
        self.eng.wait_ge(self.semaphore, self.turn * self.per_turn + self.n)


def newton_step(dve, link, var, guess, a):
    link(dve.tensor_tensor(a[:], guess[:], guess[:], ALU.mult))
    link(dve.tensor_tensor(a[:], a[:], var[:], ALU.mult))
    link(dve.tensor_scalar(a[:], a[:], -0.5, 1.5, ALU.mult, ALU.add))
    link(dve.tensor_tensor(guess[:], guess[:], a[:], ALU.mult))


def layer_norm(dve, link, out, src, tmp, settled):
    stats, mv, var, guess, a = tmp
    tiles = src.shape[1]
    for t in range(tiles):
        last = dve.bn_stats(stats[:, t], src[:, t])
    link(last)
    settled()
    for t in range(tiles):
        last = dve.bn_aggr(mv[:, t], stats[:, t])
    link(last)
    link(dve.tensor_scalar(var[:], mv[:, :, 1], EPS, None, ALU.add))
    link(dve.tensor_scalar(guess[:].bitcast(I32), var[:].bitcast(I32), 1, None, ALU.arith_shift_right))
    link(dve.tensor_scalar(guess[:].bitcast(I32), guess[:].bitcast(I32), -1.0, float(0x5F3759DF), ALU.mult, ALU.add))
    for _ in range(RSQRT_STEPS):
        newton_step(dve, link, var, guess, a)
    for t in range(tiles):
        last = dve.tensor_scalar(out[:, t], src[:, t], mv[:, t, 0:1], guess[:, t:t + 1], ALU.subtract, ALU.mult)
    link(last)


NORM_STAGES = 9
NORM_STARTS = [0, 0, 1, 5, 9, 13, 17, 21, 21]
NORM_LINKS = 22


def norm_stage(dve, chain, turn, before, stage, out, src, tmp, settled):
    stats, mv, var, guess, a = tmp
    link = Links(dve, chain, turn, 2 * NORM_LINKS)
    link.n = before + NORM_STARTS[stage]
    if stage < 2:
        for t in range(4 * stage, 4 * stage + 4):
            last = dve.bn_stats(stats[:, t], src[:, t])
        if stage == 1:
            link(last)
            settled()
    elif stage == 2:
        for t in range(NT):
            last = dve.bn_aggr(mv[:, t], stats[:, t])
        link(last)
        link(dve.tensor_scalar(var[:], mv[:, :, 1], EPS, None, ALU.add))
        link(dve.tensor_scalar(guess[:].bitcast(I32), var[:].bitcast(I32), 1, None, ALU.arith_shift_right))
        link(dve.tensor_scalar(guess[:].bitcast(I32), guess[:].bitcast(I32), -1.0, float(0x5F3759DF), ALU.mult, ALU.add))
    elif stage < 3 + RSQRT_STEPS:
        newton_step(dve, link, var, guess, a)
    else:
        for t in range(4 * (stage - 7), 4 * (stage - 7) + 4):
            last = dve.tensor_scalar(out[:, t], src[:, t], mv[:, t, 0:1], guess[:, t:t + 1], ALU.subtract, ALU.mult)
        if stage == 8:
            link(last)


def route(nc, consts, rows, y_rows, slot_info):
    with ExitStack() as ctx:
        def sb(name, shape, dt=F32):
            return ctx.enter_context(nc.sbuf_tensor("r_" + name, shape, dt))

        def sem(name):
            return ctx.enter_context(nc.semaphore("r_" + name))

        def psum(name):
            return ctx.enter_context(nc.psum_tensor("r_" + name, [P, 512], F32))

        ident = sb("ident", [P, P])
        gate_w = sb("gate_w", [P, NC, EXPERTS])
        bias = sb("bias", [P, EXPERTS])
        lower = sb("lower", [P, GROUPS_R * GROUPS_R])
        tri = sb("tri", [P, P], BF16)
        ones = sb("ones", [P, P], BF16)
        token = sb("token", [P, B * NT * 4], BF16)
        zeros = sb("zeros", [P, BLOCKS * 3], BF16)
        slot_c = sb("slot_c", [P, SLOTS, EXPERTS], BF16)
        ws_in = sb("ws_in", [P, 2, NC, FF])
        ws_down = sb("ws_down", [FF, HID])
        x2 = sb("x2", [P, NT, HID])
        row_w = sb("row_w", [P, NT, EXPERTS])
        x2T = sb("x2T", [P, NC, SEQ])
        th, score, biased, masked, replaced, selected, weight, taken = (
            sb(n, [P, NT, EXPERTS]) for n in ("th", "score", "biased", "masked", "replaced", "selected", "weight", "taken"))
        hi1, lo1 = sb("hi1", [P, NT * GROUPS_R, 4]), sb("lo1", [P, NT * GROUPS_R, 4])
        hi2, mid2, lo2 = (sb(n, [P, NT * GROUPS_R, 2]) for n in ("hi2", "mid2", "lo2"))
        hi3, mid3, lo3, group_score, group_rank = (sb(n, [P, NT * GROUPS_R]) for n in
                                                   ("hi3", "mid3", "lo3", "group_score", "group_rank"))
        at_least, above = (sb(n, [P, NT, GROUPS_R * GROUPS_R]) for n in ("at_least", "above"))
        top8 = sb("top8", [P, NT, 8])
        weight_sum, weight_inv = sb("weight_sum", [P, NT]), sb("weight_inv", [P, NT])
        selected_bf = sb("selected_bf", [P, NT, EXPERTS], BF16)
        before = sb("before", [P, EXPERTS])
        here = sb("here", [P, EXPERTS])
        before_bf = sb("before_bf", [P, EXPERTS], BF16)
        position = sb("position", [P, NT, EXPERTS], BF16)
        one_hot = sb("one_hot", [P, 2, SLOTS, EXPERTS], BF16)
        th_s, act_s = sb("th_s", [FF, SEQ]), sb("act_s", [FF, SEQ])
        h_s = sb("h_s", [FF, SEQ])
        y_s = sb("y_s", [P, NT, HID])
        info = sb("info", [P, BLOCKS, 3])

        t_ps = [psum("t_ps0"), psum("t_ps1")]
        logit_ps, count_ps, info_ps, gate_ps, up_ps, down_ps = (psum(n) for n in
                                                                ("logit", "count", "info_ps", "gate_ps", "up_ps", "down_ps"))

        first_in, late_in = sem("first_in"), sem("late_in")
        x2_in, row_out, y_out = sem("x2_in"), sem("row_out"), sem("y_out")
        select_chain, place_chain = sem("select_chain"), sem("place_chain")
        zeroed, waited = sem("zeroed"), sem("waited")
        row_done, t_ready, t_read = sem("row_done"), sem("t_ready"), sem("t_read")
        logits_ready, tanh_done = sem("logits_ready"), sem("tanh_done")
        selected_done, count_ready, hot_done, hot_used = sem("selected_done"), sem("count_ready"), sem("hot_done"), sem("hot_used")
        gate_ready, up_ready, gate_tanh, h_done, down_ready, down_read = (
            sem(n) for n in ("gate_ready", "up_ready", "gate_tanh", "h_done", "down_ready", "down_read"))
        info_read, info_out = sem("info_read"), sem("info_out")

        block = ctx.enter_context(nc.Block())
        FIRST = ((ident, "ident"), (gate_w, "gate_w"), (bias, "bias"), (ws_in, "ws_in"), (lower, "lower"))
        LATE = ((ones, "ones"), (tri, "tri"), (ws_down, "ws_down"), (token, "token"), (slot_c, "slot_c"))
        HALVES = SEQ // 512
        T_UNITS, D_UNITS = 2 * NC, NT // 2

        def later(b):
            return not isinstance(b, int) or b > 0

        def batch_rows(table, b):
            at = slice(b * SEQ, (b + 1) * SEQ) if isinstance(b, int) else bass.ds(b * SEQ, SEQ)
            return table[at]

        tiles = lambda a: a.rearrange("(t p) n -> p t n", p=P)

        def program(eng, begin, place, rest):
            begin(0)
            rest(0)
            with eng.Fori(0, B - 1) as b:
                begin(b + 1)
                place(b)
                rest(b + 1)
            place(B - 1)

        @block.sync
        def _(sp):
            def load(b):
                sp.dma_start(x2[:], tiles(batch_rows(rows, b)[:, 0:HID])).then_inc(x2_in, 16)

            def store(b):
                sp.wait_ge(down_read, b * D_UNITS + D_UNITS)
                sp.dma_start(tiles(batch_rows(y_rows, b)), y_s[:]).then_inc(y_out, 16)
                sp.wait_ge(row_done, b + 1)
                sp.dma_start(tiles(batch_rows(rows, b)[:, HID:ROW]), row_w[:]).then_inc(row_out, 16)

            load(0)
            for dst, name in FIRST:
                sp.dma_start(dst[:], consts[name]).then_inc(first_in, 16)
            for dst, name in LATE:
                sp.dma_start(dst[:], consts[name]).then_inc(late_in, 16)
            with sp.Fori(0, B - 1) as b:
                sp.wait_ge(t_ready, b * T_UNITS + T_UNITS)
                load(b + 1)
                store(b)
            store(B - 1)
            sp.wait_ge(info_read, 1)
            sp.dma_start(slot_info, info[:]).then_inc(info_out, 16)
            for s, n in ((row_out, B), (y_out, B), (info_out, 1)):
                sp.wait_ge(s, 16 * n)

        @block.vector
        def _(dve):
            def settled():
                dve.sem_inc(waited, 1)

            def shared(b, link, half):
                cols = slice(512 * half, 512 * half + 512)
                dve.wait_ge(gate_tanh, b * HALVES + half + 1)
                link(dve.scalar_tensor_tensor(act_s[:, cols], th_s[:, cols], 1.0, gate_ps[0:FF], ALU.add, ALU.mult))
                dve.wait_ge(up_ready, b * HALVES + half + 1)
                if later(b):
                    dve.wait_ge(down_ready, b * D_UNITS)
                dve.scalar_tensor_tensor(h_s[:, cols], act_s[:, cols], 0.5, up_ps[0:FF], ALU.mult, ALU.mult).then_inc(h_done, 1)

            def select(b):
                link = Links(dve, select_chain, b, SELECT_LINKS)
                dve.wait_ge(tanh_done, b + 1)
                link(dve.tensor_scalar(score[:], th[:], 0.5, 0.5, ALU.mult, ALU.add))
                link(dve.tensor_tensor(biased[:], score[:], bias[:].unsqueeze(1).broadcast_to([P, NT, EXPERTS]), ALU.add))
                v8 = biased[:].rearrange("p t (g n) -> p (t g) n", g=GROUPS_R)
                dve.tensor_tensor(hi1[:], v8[:, :, 0:4], v8[:, :, 4:8], ALU.max)
                link(dve.tensor_tensor(lo1[:], v8[:, :, 0:4], v8[:, :, 4:8], ALU.min))
                dve.tensor_tensor(hi2[:], hi1[:, :, 0:2], hi1[:, :, 2:4], ALU.max)
                dve.tensor_tensor(mid2[:], hi1[:, :, 0:2], hi1[:, :, 2:4], ALU.min)
                link(dve.tensor_tensor(lo2[:], lo1[:, :, 0:2], lo1[:, :, 2:4], ALU.max))
                link(dve.tensor_tensor(lo2[:], lo2[:], mid2[:], ALU.max))
                dve.tensor_tensor(hi3[:], hi2[:, :, 0], hi2[:, :, 1], ALU.max)
                dve.tensor_tensor(mid3[:], hi2[:, :, 0], hi2[:, :, 1], ALU.min)
                link(dve.tensor_tensor(lo3[:], lo2[:, :, 0], lo2[:, :, 1], ALU.max))
                link(dve.tensor_tensor(lo3[:], lo3[:], mid3[:], ALU.max))
                link(dve.tensor_tensor(group_score[:], hi3[:], lo3[:], ALU.add))

                shared(b, link, 0)

                gs = group_score[:].rearrange("p (t g) -> p t g", t=NT)
                other = gs.unsqueeze(2).broadcast_to([P, NT, GROUPS_R, GROUPS_R])
                own = gs.unsqueeze(3).broadcast_to([P, NT, GROUPS_R, GROUPS_R])
                square = lambda a: a[:].rearrange("p t (g h) -> p t g h", g=GROUPS_R)
                dve.tensor_tensor(square(at_least), other, own, ALU.is_ge)
                link(dve.tensor_tensor(square(above), other, own, ALU.is_gt))
                link(dve.tensor_tensor(at_least[:], at_least[:], above[:], ALU.subtract))
                link(dve.tensor_tensor(at_least[:], at_least[:], lower[:].unsqueeze(1).broadcast_to([P, NT, 64]), ALU.mult))
                link(dve.tensor_tensor(at_least[:], at_least[:], above[:], ALU.add))
                link(dve.tensor_reduce(group_rank[:].rearrange("p (t g) -> p t g", t=NT), square(at_least), AX.X, ALU.add))
                link(dve.tensor_scalar(group_rank[:], group_rank[:], TOP_GROUPS - 0.5, NEG, ALU.is_gt, ALU.mult))
                link(dve.tensor_tensor(masked[:].rearrange("p t (g n) -> p (t g) n", g=GROUPS_R), v8,
                                       group_rank[:].unsqueeze(2).broadcast_to([P, NT * GROUPS_R, 8]), ALU.add))
                shared(b, link, 1)
                settled()
                for t in range(NT):
                    last = dve.max(top8[:, t], masked[:, t])
                link(last)
                link(dve.memset(top8[:, :, TOP:8], NEG))
                settled()
                for t in range(NT):
                    last = dve.match_replace(replaced[:, t], top8[:, t], masked[:, t], NEG)
                link(last)
                link(dve.tensor_tensor(selected[:], masked[:], replaced[:], ALU.not_equal))
                dve.tensor_copy(selected_bf[:], selected[:]).then_inc(selected_done, 1)
                link(dve.tensor_tensor(weight[:], score[:], selected[:], ALU.mult))
                link(dve.tensor_reduce(weight_sum[:], weight[:], AX.X, ALU.add))
                link(dve.reciprocal(weight_inv[:], weight_sum[:]))
                link(dve.tensor_scalar(weight_inv[:], weight_inv[:], SCALE, None, ALU.mult))
                if later(b):
                    dve.wait_ge(row_out, b * 16)
                dve.tensor_tensor(row_w[:], weight[:], weight_inv[:].unsqueeze(2).broadcast_to([P, NT, EXPERTS]),
                                  ALU.mult).then_inc(row_done, 1)
                assert link.n == SELECT_LINKS, link.n

            def place(b):
                link = Links(dve, place_chain, b, PLACE_LINKS)
                link(dve.tensor_scalar(taken[:], selected[:], -4096.0, 4096.0, ALU.mult, ALU.add))
                dve.wait_ge(count_ready, b + 1)
                dve.tensor_tensor(position[:], count_ps[:].rearrange("p (t e) -> p t e", t=NT), taken[:], ALU.add)
                link(dve.tensor_reduce(here[:], selected[:].rearrange("p t e -> p e t"), AX.X, ALU.add))
                link(dve.tensor_tensor(before[:], before[:], here[:], ALU.add))
                link(dve.tensor_copy(before_bf[:], before[:]))
                for t in range(NT):
                    if t >= 2:
                        dve.wait_ge(hot_used, b * NT + t - 1)
                    dve.tensor_tensor(one_hot[:, t % 2], slot_c[:], position[:, t].unsqueeze(1).broadcast_to([P, SLOTS, EXPERTS]),
                                      ALU.is_equal).then_inc(hot_done, 1)
                assert link.n == PLACE_LINKS, link.n

            dve.memset(zeros[:], 0.0)
            dve.memset(before[:], 0.0)
            dve.memset(before_bf[:], 0.0).then_inc(zeroed, 1)
            dve.wait_ge(zeroed, 1)
            dve.wait_ge(first_in, 16 * len(FIRST))
            select(0)
            dve.wait_ge(late_in, 16 * len(LATE))
            with dve.Fori(0, B - 1) as b:
                place(b)
                select(b + 1)
                dve.wait_ge(hot_used, b * NT + NT)
            place(B - 1)
            dve.wait_ge(hot_used, B * NT)
            dve.tensor_copy(info[:], info_ps[:, 0:BLOCKS * 3].rearrange("p (n k) -> p n k", k=3)).then_inc(info_read, 1)

        @block.scalar
        def _(act):
            def begin(b):
                for u in range(T_UNITS):
                    c, half = u % 2, u // 2
                    act.wait_ge(t_ready, b * T_UNITS + u + 1)
                    act.activation(x2T[:, c, 512 * half:512 * half + 512], t_ps[u % 2][:], ACT.Copy).then_inc(t_read, 1)
                act.wait_ge(logits_ready, b + 1)
                act.activation(th[:], logit_ps[:].rearrange("p (t e) -> p t e", t=NT), ACT.Tanh, scale=0.5).then_inc(tanh_done, 1)

            def rest(b):
                for half in range(HALVES):
                    act.wait_ge(gate_ready, b * HALVES + half + 1)
                    act.activation(th_s[:, 512 * half:512 * half + 512], gate_ps[0:FF], ACT.Tanh, scale=0.5).then_inc(gate_tanh, 1)
                if later(b):
                    act.wait_ge(y_out, b * 16)
                for u in range(D_UNITS):
                    act.wait_ge(down_ready, b * D_UNITS + u + 1)
                    act.activation(y_s[:, 2 * u:2 * u + 2], down_ps[:].rearrange("p (t n) -> p t n", t=2), ACT.Copy).then_inc(down_read, 1)

            program(act, begin, lambda b: None, rest)

        @block.tensor
        def _(pe):
            def begin(b):
                pe.wait_ge(x2_in, b * 16 + 16)
                for u in range(T_UNITS):
                    c, half = u % 2, u // 2
                    if later(b) or u >= 2:
                        pe.wait_ge(t_read, b * T_UNITS + u - 1)
                    for i in range(4):
                        last = pe.transpose(t_ps[u % 2][:, i * P:(i + 1) * P], x2[:, 4 * half + i, c * P:(c + 1) * P], ident[:])
                    last.then_inc(t_ready, 1)
                pe.wait_ge(t_read, b * T_UNITS + T_UNITS)
                for t in range(NT):
                    for c in range(NC):
                        last = pe.matmul(logit_ps[:, t * EXPERTS:(t + 1) * EXPERTS], x2T[:, c, t * P:(t + 1) * P], gate_w[:, c],
                                         start=(c == 0), stop=(c == NC - 1))
                last.then_inc(logits_ready, 1)

            def place(b):
                for t in range(NT):
                    pe.wait_ge(hot_done, b * NT + t + 1)
                    for n in range(BLOCKS):
                        at = b * (4 * NT) + 4 * t
                        last = pe.matmul(info_ps[:, 3 * n:3 * n + 3], one_hot[:, t % 2, 2 * n:2 * n + 2].rearrange("p c e -> p (c e)"),
                                         token[:, at:at + 3] if isinstance(b, int) else token[:, bass.ds(at, 3)],
                                         start=False, stop=True, skip_group_check=True)
                    last.then_inc(hot_used, 1)

            def rest(b):
                for half in range(HALVES):
                    cols = slice(512 * half, 512 * half + 512)
                    if later(b) or half:
                        pe.wait_ge(h_done, b * HALVES + half)
                    for k, (bank, ready) in enumerate(((gate_ps, gate_ready), (up_ps, up_ready))):
                        for c in range(NC):
                            last = pe.matmul(bank[0:FF], ws_in[:, k, c], x2T[:, c, cols], start=(c == 0), stop=(c == NC - 1))
                        last.then_inc(ready, 1)
                for u in range(D_UNITS):
                    pe.wait_ge(h_done, b * HALVES + u // 2 + 1)
                    if later(b) or u:
                        pe.wait_ge(down_read, b * D_UNITS + u)
                    for i in range(2):
                        t = 2 * u + i
                        last = pe.matmul(down_ps[:, i * HID:(i + 1) * HID], h_s[:, t * P:(t + 1) * P], ws_down[:], start=True, stop=True)
                    last.then_inc(down_ready, 1)
                pe.wait_ge(selected_done, b + 1)
                for t in range(NT):
                    out = count_ps[:, t * EXPERTS:(t + 1) * EXPERTS]
                    pe.matmul(out, tri[:], selected_bf[:, t], start=True, stop=False)
                    for i in range(t):
                        pe.matmul(out, ones[:], selected_bf[:, i], start=False, stop=False)
                    last = pe.matmul(out, ones[:], before_bf[:], start=False, stop=True)
                last.then_inc(count_ready, 1)

            pe.wait_ge(first_in, 16 * len(FIRST))
            pe.wait_ge(late_in, 16 * len(LATE))
            pe.wait_ge(zeroed, 1)
            pe.matmul(info_ps[:, 0:BLOCKS * 3], ones[:], zeros[:], start=True, stop=True)
            program(pe, begin, place, rest)


def experts(nc, consts, rows, slot_info, slot_rows, slot_weights, expert_w, sums):
    with ExitStack() as ctx:
        def sb(name, shape, dt=F32):
            return ctx.enter_context(nc.sbuf_tensor("e_" + name, shape, dt))

        def sem(name):
            return ctx.enter_context(nc.semaphore("e_" + name))

        def psum(name):
            return ctx.enter_context(nc.psum_tensor("e_" + name, [P, 512], F32))

        TURN = 8
        N_TURNS = EXPERTS // TURN
        PACK_IN, PACK = 2 * NC * FF, 2 * NC * FF + HID
        GATHERS = 6

        ident = sb("ident", [P, P])
        diag = sb("diag", [P, EXPERTS])
        trash = sb("trash", [P, BLOCKS])
        info = sb("info", [P, BLOCKS, 3])
        row_f, row_i = sb("row_f", [P, BLOCKS]), sb("row_i", [P, BLOCKS], I32)
        gathered = sb("gathered", [P, BLOCKS, ROW])
        own_w = sb("own_w", [P, BLOCKS, EXPERTS])
        w_slot = sb("w_slot", [P, BLOCKS])
        rows_by_slot, w_by_slot = sb("rows_by_slot", [BLOCKS, P], I32), sb("w_by_slot", [BLOCKS, P])
        by_slot_ready, by_slot_done = sem("by_slot_ready"), sem("by_slot_done")
        xsT = sb("xsT", [P, NC, EXPERTS, SLOTS])
        dest = sb("dest", [SLOTS, EXPERTS], I32)
        w_dest = sb("w_dest", [SLOTS, EXPERTS])
        w_in = sb("w_in", [P, 2, TURN, PACK_IN])
        w_down = sb("w_down", [FF, 2, TURN, HID])
        th, a, h = (sb(n, [FF, TURN * SLOTS]) for n in ("th", "a", "h"))
        y = sb("y", [SLOTS, 2, TURN, HID])

        t_ps = [psum("t_ps0"), psum("t_ps1")]
        gate_ps, up_ps = psum("gate"), psum("up")
        y_ps = [psum("y_ps0"), psum("y_ps1")]

        consts_in, chain = sem("consts_in"), sem("chain")
        row_ready, w_ready, slots_out, dest_in = sem("row_ready"), sem("w_ready"), sem("slots_out"), sem("dest_in")
        gathered_in = [sem(f"gathered_in{i}") for i in range(BLOCKS // GATHERS)]
        wi_in = [sem(f"wi_in{i}") for i in range(2)]
        wd_in = [sem(f"wd_in{i}") for i in range(2)]
        t_ready, t_read = sem("t_ready"), sem("t_read")
        gate_ready, up_ready, tanh_done, h_done, y_ready, y_read = (
            sem(n) for n in ("gate_ready", "up_ready", "tanh_done", "h_done", "y_ready", "y_read"))
        added = [sem(f"added{i}") for i in range(2)]

        block = ctx.enter_context(nc.Block())
        UNITS_T = 2 * BLOCKS // 4

        def later(i):
            return not isinstance(i, int) or i > 0

        def column(a, i):
            return a[:, i:i + 1] if isinstance(i, int) else a[:, bass.ds(i, 1)]

        @block.sync
        def _(sp):
            for dst, src in ((ident, consts["ident"]), (diag, consts["diag"]), (trash, consts["trash"]), (info, slot_info)):
                sp.dma_start(dst[:], src).then_inc(consts_in, 16)

            def load(e, parity):
                w = expert_w[bass.ds(e, TURN)] if not isinstance(e, int) else expert_w[e:e + TURN]
                sp.dma_start(w_in[:, parity], w[:, :, 0:PACK_IN].rearrange("e p n -> p e n")).then_inc(wi_in[parity], 16)
                sp.dma_start(w_down[:, parity], w[:, 0:FF, PACK_IN:PACK].rearrange("e p n -> p e n")).then_inc(wd_in[parity], 16)

            load(0, 0)
            load(TURN, 1)
            sp.wait_ge(by_slot_done, 1)
            sp.dma_start(slot_rows.rearrange("(n p) -> n p", p=P), rows_by_slot[:]).then_inc(slots_out, 16)
            sp.wait_ge(by_slot_done, 2)
            sp.dma_start(slot_weights.rearrange("(n p) -> n p", p=P), w_by_slot[:]).then_inc(slots_out, 16)
            sp.wait_ge(slots_out, 32)
            sp.dma_start(dest[:], slot_rows.rearrange("(c e) -> c e", e=EXPERTS)).then_inc(dest_in, 16)
            sp.dma_start(w_dest[:], slot_weights.rearrange("(c e) -> c e", e=EXPERTS)).then_inc(dest_in, 16)
            with sp.Fori(0, N_TURNS // 2 - 1) as i:
                for parity in range(2):
                    sp.wait_ge(y_ready, i * TURN + (parity + 1) * (TURN // 2))
                    load(i * (2 * TURN) + (2 + parity) * TURN, parity)

        @block.gpsimd
        def _(pool):
            pool.wait_ge(row_ready, 1)
            for n in range(BLOCKS):
                pool.indirect_dma_start(gathered[:, n], None, rows, bass.IndirectOffsetOnAxis(row_i[:, n:n + 1], 0),
                                        bounds_check=TOKENS + TRASH - 1, oob_is_err=False).then_inc(gathered_in[n // GATHERS], 16)
            pool.wait_ge(dest_in, 32)
            for e in range(EXPERTS):
                if e % 2 == 0:
                    pool.wait_ge(y_read, e // 2 + 1)
                if e >= 2:
                    pool.wait_ge(added[e % 2], 16 * (e // 2))
                pool.indirect_dma_start(sums[e % 2], bass.IndirectOffsetOnAxis(dest[:, e:e + 1], 0), y[:, (e // TURN) % 2, e % TURN], None,
                                        bounds_check=TOKENS + TRASH - 1, compute_op=ALU.add).then_inc(added[e % 2], 16)
            for i in range(2):
                pool.wait_ge(added[i], 16 * EXPERTS // 2)

        @block.vector
        def _(dve):
            link = Links(dve, chain, 0, 0)
            dve.wait_ge(consts_in, 4 * 16)
            link(dve.scalar_tensor_tensor(row_f[:], info[:, :, 1], float(P), info[:, :, 0], ALU.mult, ALU.add))
            link(dve.tensor_tensor(row_f[:], row_f[:], trash[:], ALU.subtract))
            link(dve.tensor_tensor(row_f[:], row_f[:], info[:, :, 2], ALU.mult))
            link(dve.tensor_tensor(row_f[:], row_f[:], trash[:], ALU.add))
            dve.tensor_copy(row_i[:], row_f[:]).then_inc(row_ready, 1)
            dve.wait_ge(by_slot_ready, 1)
            dve.tensor_copy(rows_by_slot[:], gate_ps[0:BLOCKS, 0:P]).then_inc(by_slot_done, 1)
            for g in range(BLOCKS // GATHERS):
                dve.wait_ge(gathered_in[g], 16 * GATHERS)
            link(dve.tensor_tensor(own_w[:], gathered[:, :, HID:ROW], diag[:].unsqueeze(1).broadcast_to([P, BLOCKS, EXPERTS]), ALU.mult))
            dve.tensor_reduce(w_slot[:], own_w[:], AX.X, ALU.add).then_inc(w_ready, 1)
            dve.wait_ge(by_slot_ready, 2)
            dve.tensor_copy(w_by_slot[:], up_ps[0:BLOCKS, 0:P]).then_inc(by_slot_done, 1)

            def hidden(i):
                dve.wait_ge(tanh_done, i + 1)
                dve.scalar_tensor_tensor(a[:], th[:], 1.0, gate_ps[0:FF, 0:TURN * SLOTS], ALU.add, ALU.mult).then_inc(chain, 1)
                dve.wait_ge(chain, i + 6)
                dve.wait_ge(up_ready, i + 1)
                if later(i):
                    dve.wait_ge(y_ready, i * (TURN // 2))
                dve.scalar_tensor_tensor(h[:], a[:], 0.5, up_ps[0:FF, 0:TURN * SLOTS], ALU.mult, ALU.mult).then_inc(h_done, 1)

            hidden(0)
            with dve.Fori(0, N_TURNS - 1) as i:
                hidden(i + 1)

        @block.scalar
        def _(act):
            for u in range(UNITS_T):
                act.wait_ge(t_ready, u + 1)
                c, n = u % 2, 4 * (u // 2)
                act.activation(xsT[:, c, :, 2 * n:2 * n + 8].rearrange("p e c -> p c e"),
                               t_ps[u % 2][:].rearrange("p (c e) -> p c e", e=EXPERTS), ACT.Copy).then_inc(t_read, 1)
            act.wait_ge(dest_in, 32)

            def two_turns(i):
                for parity in range(2):
                    act.wait_ge(gate_ready, i * 2 + parity + 1)
                    if later(i) or parity:
                        act.wait_ge(h_done, i * 2 + parity)
                    act.activation(th[:], gate_ps[0:FF, 0:TURN * SLOTS], ACT.Tanh, scale=0.5).then_inc(tanh_done, 1)
                    if later(i):
                        for q in range(2):
                            act.wait_ge(added[q], i * (16 * TURN))
                    for u in range(TURN // 2):
                        act.wait_ge(y_ready, i * TURN + parity * (TURN // 2) + u + 1)
                        for q in range(2):
                            last = act.activation(y[:, parity, 2 * u + q], y_ps[u % 2][0:SLOTS, q * HID:(q + 1) * HID], ACT.Copy,
                                                  scale=column(w_dest, i * (2 * TURN) + parity * TURN + 2 * u + q))
                        last.then_inc(y_read, 1)

            two_turns(0)
            with act.Fori(0, N_TURNS // 2 - 1) as i:
                two_turns(i + 1)

        @block.tensor
        def _(pe):
            pe.wait_ge(consts_in, 4 * 16)
            pe.wait_ge(row_ready, 1)
            pe.transpose(gate_ps[0:BLOCKS, 0:P], row_f[:], ident[:]).then_inc(by_slot_ready, 1)
            for u in range(UNITS_T):
                c, n = u % 2, 4 * (u // 2)
                for g in range((n + 3) // GATHERS + 1):
                    pe.wait_ge(gathered_in[g], 16 * GATHERS)
                if u >= 2:
                    pe.wait_ge(t_read, u - 1)
                for k in range(4):
                    last = pe.transpose(t_ps[u % 2][:, k * P:(k + 1) * P], gathered[:, n + k, c * P:(c + 1) * P], ident[:])
                last.then_inc(t_ready, 1)
            pe.wait_ge(w_ready, 1)
            pe.transpose(up_ps[0:BLOCKS, 0:P], w_slot[:], ident[:]).then_inc(by_slot_ready, 1)
            pe.wait_ge(t_read, UNITS_T)
            pe.wait_ge(by_slot_done, 2)

            def two_turns(i):
                for parity in range(2):
                    pe.wait_ge(wi_in[parity], i * 16 + 16)
                    if later(i) or parity:
                        pe.wait_ge(h_done, i * 2 + parity)
                    for k, (bank, ready) in enumerate(((gate_ps, gate_ready), (up_ps, up_ready))):
                        for e in range(TURN):
                            for c in range(NC):
                                col = (k * NC + c) * FF
                                slots = column(xsT[:, c], i * (2 * TURN) + parity * TURN + e).rearrange("p e c -> p (e c)")
                                last = pe.matmul(bank[0:FF, e * SLOTS:(e + 1) * SLOTS], w_in[:, parity, e, col:col + FF], slots,
                                                 start=(c == 0), stop=(c == NC - 1))
                        last.then_inc(ready, 1)
                    pe.wait_ge(wd_in[parity], i * 16 + 16)
                    pe.wait_ge(h_done, i * 2 + parity + 1)
                    for u in range(TURN // 2):
                        if later(i) or parity or u >= 2:
                            pe.wait_ge(y_read, i * TURN + parity * (TURN // 2) + u - 1)
                        for q in range(2):
                            e = 2 * u + q
                            last = pe.matmul(y_ps[u % 2][0:SLOTS, q * HID:(q + 1) * HID], h[:, e * SLOTS:(e + 1) * SLOTS],
                                             w_down[:, parity, e], start=True, stop=True)
                        last.then_inc(y_ready, 1)

            two_turns(0)
            with pe.Fori(0, N_TURNS // 2 - 1) as i:
                two_turns(i + 1)


def finish(nc, x1_rows, sums, out):
    with ExitStack() as ctx:
        def sb(name, shape, dt=F32):
            return ctx.enter_context(nc.sbuf_tensor("f_" + name, shape, dt))

        def sem(name):
            return ctx.enter_context(nc.semaphore("f_" + name))

        x1, m0, m1 = (sb(n, [P, B, NT, HID]) for n in ("x1", "m0", "m1"))
        tmp = (sb("stats", [P, NT, 6]), sb("mv", [P, NT, 2]), sb("var", [P, NT]), sb("guess", [P, NT]), sb("newton", [P, NT]))
        loaded = [sem(f"loaded{b}") for b in range(B)]
        summed, chain, done, stored = sem("summed"), sem("chain"), sem("done"), sem("stored")
        block = ctx.enter_context(nc.Block())
        tiles = lambda a: a.rearrange("(t p) n -> p t n", p=P)

        @block.sync
        def _(sp):
            for b in range(B):
                sp.dma_start(m0[:, b], tiles(sums[0][b * SEQ:(b + 1) * SEQ])).then_inc(loaded[b], 16)
                sp.dma_start(m1[:, b], tiles(sums[1][b * SEQ:(b + 1) * SEQ])).then_inc(loaded[b], 16)
                sp.dma_start(x1[:, b], x1_rows[b]).then_inc(loaded[b], 16)
            for b in range(B):
                sp.wait_ge(done, b + 1)
                sp.dma_start(out[b].rearrange("(t p) n -> p t n", p=P), x1[:, b]).then_inc(stored, 16)
            sp.wait_ge(stored, 16 * B)

        @block.gpsimd
        def _(pool):
            for b in range(B):
                pool.wait_ge(loaded[b], 48)
                pool.tensor_tensor(m0[:, b], m0[:, b], m1[:, b], ALU.add).then_inc(summed, 1)

        @block.vector
        def _(dve):
            link = Links(dve, chain, 0, 0)
            for b in range(B):
                dve.wait_ge(summed, b + 1)
                layer_norm(dve, link, m0[:, b], m0[:, b], tmp, lambda: None)
                dve.tensor_tensor(x1[:, b], x1[:, b], m0[:, b], ALU.add).then_inc(done, 1)


def build(nc, args, out):
    x, wpack = args["x"], args["wpack"]
    w_split = nc.dram_tensor("w_split", (KV_HEADS, P, 2 * WPACK), F32).ap()
    xT_split = nc.dram_tensor("xT_split", (B, P, 2 * NC * SEQ), F32).ap()
    x1_rows = nc.dram_tensor("x1_rows", (B, P, NT, HID), F32).ap()
    rows = nc.dram_tensor("rows", (TOKENS + TRASH, ROW), F32).ap()
    sums = [nc.dram_tensor(f"sums{i}", (TOKENS + TRASH, HID), F32).ap() for i in range(2)]
    slot_info = nc.dram_tensor("slot_info", (P, BLOCKS, 3), F32).ap()
    slot_rows = nc.dram_tensor("slot_rows", (EXPERTS * SLOTS,), I32).ap()
    slot_weights = nc.dram_tensor("slot_weights", (EXPERTS * SLOTS,), F32).ap()
    prepare(nc, x, wpack, args, w_split, xT_split, rows, sums)
    attention(nc, args, x, w_split, xT_split, x1_rows, rows)
    route(nc, args, rows, sums[0], slot_info)
    experts(nc, args, rows, slot_info, slot_rows, slot_weights, args["expert_w"], sums)
    finish(nc, x1_rows, sums, out)


def lay_out(inputs):
    f = lambda n: np.asarray(inputs[n])
    wq, wk, wv, wo = (f("L0_attn_" + n) for n in ("Wq", "Wk", "Wv", "Wo"))

    def halves(w):
        return w.reshape(-1, HD // 2, 2, HID).transpose(0, 2, 1, 3).reshape(-1, HD, HID)

    q, k, v_ = halves(wq), halves(wk), wv.reshape(KV_HEADS, HD, HID)
    packs = []
    for g in range(KV_HEADS):
        a = np.stack([k[g], v_[g], q[4 * g], q[4 * g + 1]])
        b = q[4 * g + 2:4 * g + 4]
        at = a.reshape(-1, NC, P).transpose(2, 1, 0).reshape(P, -1)
        bt = b.reshape(-1, NC, P).transpose(2, 1, 0).reshape(P, -1)
        o = wo[:, 512 * g:512 * g + 512].reshape(HID, GROUP, HD).transpose(2, 1, 0).reshape(P, -1)
        packs.append(np.concatenate([at, bt, o], 1))
    arrays = {"x": f("L0_attn_x"), "wpack": np.stack(packs)}
    freq = np.float32(1) / np.power(10000.0, np.arange(0, HD, 2) / HD).astype(np.float32)
    angle = (np.arange(SEQ, dtype=np.float32)[:, None] * freq[None]).astype(np.float64)
    s = float(HD) ** -0.25
    cos = np.concatenate([np.cos(angle), np.cos(angle)], 1) * s
    sin = np.concatenate([np.sin(angle), -np.sin(angle)], 1) * s
    lay = lambda a: np.ascontiguousarray(a.reshape(NT, P, HD).transpose(1, 0, 2)).astype(np.float32)
    arrays["cos"], arrays["sin"] = lay(cos), lay(sin)
    arrays["ident"] = np.eye(P, dtype=np.float32)
    arrays["ident_bf"] = np.eye(P).astype(mybir.dt.np(BF16))
    arrays["mask_bf"] = np.triu(np.full((P, P), NEG), 1).astype(mybir.dt.np(BF16))
    g = lambda n: np.asarray(inputs["L0_ffn_" + n])
    chunks = lambda w: w.reshape(NC, P, -1).transpose(1, 0, 2)
    arrays["gate_w"] = chunks(g("gate_w"))
    arrays["bias"] = np.broadcast_to(g("bias"), (P, EXPERTS))
    arrays["ws_in"] = np.stack([chunks(g("ws_gate")), chunks(g("ws_up"))], 1)
    arrays["ws_down"] = g("ws_down")
    w_in = np.stack([g("w_gate"), g("w_up")], 1).reshape(EXPERTS, 2, NC, P, FF).transpose(0, 3, 1, 2, 4).reshape(EXPERTS, P, -1)
    w_down = np.concatenate([g("w_down"), np.zeros((EXPERTS, P - FF, HID), np.float32)], 1)
    arrays["expert_w"] = np.concatenate([w_in, w_down], 2)
    bf = mybir.dt.np(BF16)
    lower = np.arange(GROUPS_R)[None] < np.arange(GROUPS_R)[:, None]
    arrays["lower"] = np.broadcast_to(lower.reshape(-1), (P, GROUPS_R ** 2)).astype(np.float32)
    arrays["tri"] = np.triu(np.ones((P, P)), 1).astype(bf)
    arrays["ones"] = np.ones((P, P)).astype(bf)
    p, t = np.meshgrid(np.arange(P), np.arange(B * NT), indexing="ij")
    arrays["token"] = np.stack([p, t, np.ones_like(p), np.zeros_like(p)], 2).reshape(P, -1).astype(bf)
    arrays["slot_c"] = np.broadcast_to(np.arange(SLOTS)[None, :, None], (P, SLOTS, EXPERTS)).astype(bf)
    arrays["diag"] = (np.arange(P)[:, None] % EXPERTS == np.arange(EXPERTS)[None]).astype(np.float32)
    arrays["trash"] = (TOKENS + 2 * np.arange(BLOCKS)[None] + np.arange(P)[:, None] // EXPERTS).astype(np.float32)
    return {n: np.ascontiguousarray(a) for n, a in arrays.items()}


def kernel(**inputs):
    import concourse.bacc as _bacc
    from concourse.bass_utils import run_bass_kernel_spmd as _run

    nc = _bacc.Bacc("TRN2", target_bir_lowering=False, num_devices=1)
    arrays = lay_out(inputs)
    args = {n: nc.dram_tensor(f"in_{n}", a.shape, mybir.dt.from_np(a.dtype), kind="ExternalInput").ap()
            for n, a in arrays.items()}
    out = nc.dram_tensor("out", (B, SEQ, HID), F32, kind="ExternalOutput").ap()
    build(nc, args, out)
    r = _run(nc, [{f"in_{n}": a for n, a in arrays.items()}], core_ids=[0])
    return np.asarray(r.results[0]["out"])
```
